# Optimizing a Trainium2 kernel written in Bass

```python
import numpy as np
import jax
import jax.numpy as jnp

def _softmax(x, axis=-1):
    return jax.nn.softmax(x, axis=axis)

def _gelu(x):
    return jax.nn.gelu(x, approximate=True)

def _silu(x):
    return jax.nn.silu(x)

def _sigmoid(x):
    return jax.nn.sigmoid(x)

def _layernorm(x, axis=-1, eps=1e-05):
    m = jnp.mean(x, axis=axis, keepdims=True)
    v = jnp.var(x, axis=axis, keepdims=True)
    return (x - m) / jnp.sqrt(v + eps)

def _scatter_add(tgt, idx, src, axis=0):
    return tgt.at[idx].add(src)

def _segment_sum(src, seg, n):
    return jax.ops.segment_sum(src, seg, n)
kernel_name = 'mk_adj_resnorm_d2_adj_r2_7f14fb'

def setup_inputs(seed: int=0):
    np.random.seed(seed)
    _w = jnp.asarray

    def _rec_inputs():
        import jax
        import jax.numpy as jnp
        _gk = jax.random.key(seed)
        x = 7.22e-05 + 1 * jax.random.normal(jax.random.fold_in(_gk, 1), (32, 256, 256), jnp.float32)
        _a = jax.random.bernoulli(jax.random.fold_in(_gk, 2), 0.0625, (32, 256, 256))
        adj = _a.astype(jnp.int32)
        return (x, adj)
    x, adj = _rec_inputs()

    def _L0_gnn_setup():
        import jax, jax.numpy as jnp
        import numpy as np
        ALPHA = 0.2
        MASK_VAL = -1000000000.0
        key = jax.random.key(seed)
        k1, k2, k3, k4 = jax.random.split(key, 4)
        B, N, F_in, F_out = (8, 1024, 256, 256)
        h = jax.random.normal(k1, (B, N, F_in), dtype=jnp.float32)
        adj = jax.random.randint(k2, (B, N, N), 0, 2, dtype=jnp.int32)

        def xavier(k, shape, gain=1.414):
            fan_in, fan_out = (shape[0], shape[1])
            bound = gain * np.sqrt(6.0 / (fan_in + fan_out))
            return jax.random.uniform(k, shape, jnp.float32, -bound, bound)
        W = xavier(k3, (F_in, F_out))
        a = xavier(k4, (2 * F_out, 1))
        return {'h': h, 'adj': adj, 'W': W, 'a': a}
    _L0_gnn_all = _L0_gnn_setup()
    _L0_gnn_in = {k: v for k, v in _L0_gnn_all.items() if k in ('W', 'a')}
    del _L0_gnn_all

    def _L1_gnn_setup():
        import jax, jax.numpy as jnp
        import numpy as np
        NEG_INF = -1000000000.0
        NEG_SLOPE = 0.2

        def gat_layer(x, mask, W, a_src, a_dst, bias, concat):
            B, N, _ = x.shape
            H, F = a_src.shape
            xl = (x @ W).reshape(B, N, H, F)
            asrc = jnp.einsum('bnhf,hf->bnh', xl, a_src)
            adst = jnp.einsum('bnhf,hf->bnh', xl, a_dst)
            e = jax.nn.leaky_relu(asrc[:, :, None, :] + adst[:, None, :, :], NEG_SLOPE)
            e = jnp.where(mask[..., None], e, NEG_INF)
            attn = jax.nn.softmax(e, axis=1)
            out = jnp.einsum('bsdh,bshf->bdhf', attn, xl)
            if concat:
                out = out.reshape(B, N, H * F)
            else:
                out = out.mean(axis=2)
            return out + bias
        key = jax.random.key(seed)
        ks = jax.random.split(key, 10)
        B, N, Din, Fh, H, Dout = (8, 512, 256, 128, 4, 256)
        s = 0.05
        return {'adj': jax.random.randint(ks[0], (B, N, N), 0, 2, dtype=jnp.int32), 'x': jax.random.normal(ks[1], (B, N, Din), dtype=jnp.float32), 'W1': jax.random.normal(ks[2], (Din, H * Fh), dtype=jnp.float32) * s, 'att_src1': jax.random.normal(ks[3], (H, Fh), dtype=jnp.float32) * s, 'att_dst1': jax.random.normal(ks[4], (H, Fh), dtype=jnp.float32) * s, 'b1': jax.random.normal(ks[5], (H * Fh,), dtype=jnp.float32) * s, 'W2': jax.random.normal(ks[6], (H * Fh, Dout), dtype=jnp.float32) * s, 'att_src2': jax.random.normal(ks[7], (1, Dout), dtype=jnp.float32) * s, 'att_dst2': jax.random.normal(ks[8], (1, Dout), dtype=jnp.float32) * s, 'b2': jax.random.normal(ks[9], (Dout,), dtype=jnp.float32) * s}
    _L1_gnn_all = _L1_gnn_setup()
    _L1_gnn_in = {k: v for k, v in _L1_gnn_all.items() if k in ('W1', 'att_src1', 'att_dst1', 'b1', 'W2', 'att_src2', 'att_dst2', 'b2')}
    del _L1_gnn_all
    return {'x': x, 'adj': adj, 'L0_gnn_W': _L0_gnn_in['W'], 'L0_gnn_a': _L0_gnn_in['a'], 'L1_gnn_W1': _L1_gnn_in['W1'], 'L1_gnn_att_src1': _L1_gnn_in['att_src1'], 'L1_gnn_att_dst1': _L1_gnn_in['att_dst1'], 'L1_gnn_b1': _L1_gnn_in['b1'], 'L1_gnn_W2': _L1_gnn_in['W2'], 'L1_gnn_att_src2': _L1_gnn_in['att_src2'], 'L1_gnn_att_dst2': _L1_gnn_in['att_dst2'], 'L1_gnn_b2': _L1_gnn_in['b2']}

def reference(x, adj, L0_gnn_W, L0_gnn_a, L1_gnn_W1, L1_gnn_att_src1, L1_gnn_att_dst1, L1_gnn_b1, L1_gnn_W2, L1_gnn_att_src2, L1_gnn_att_dst2, L1_gnn_b2):
    import jax
    import jax.numpy as jnp

    def _L0_gnn_ref(h, adj, W, a):
        import jax, jax.numpy as jnp
        import numpy as np
        ALPHA = 0.2
        MASK_VAL = -1000000000.0
        Fout = W.shape[1]
        Wh = jnp.matmul(h, W)
        a1 = a[:Fout, 0]
        a2 = a[Fout:, 0]
        e_i = jnp.einsum('bnf,f->bn', Wh, a1)
        e_j = jnp.einsum('bnf,f->bn', Wh, a2)
        e = e_i[:, :, None] + e_j[:, None, :]
        e = jax.nn.leaky_relu(e, negative_slope=ALPHA)
        e = jnp.where(adj == 0, MASK_VAL, e)
        attention = jax.nn.softmax(e, axis=2)
        h_prime = jnp.matmul(attention, Wh)
        return jax.nn.elu(h_prime)

    def _L1_gnn_ref(adj, x, W1, att_src1, att_dst1, b1, W2, att_src2, att_dst2, b2):
        import jax, jax.numpy as jnp
        import numpy as np
        NEG_INF = -1000000000.0
        NEG_SLOPE = 0.2

        def gat_layer(x, mask, W, a_src, a_dst, bias, concat):
            B, N, _ = x.shape
            H, F = a_src.shape
            xl = (x @ W).reshape(B, N, H, F)
            asrc = jnp.einsum('bnhf,hf->bnh', xl, a_src)
            adst = jnp.einsum('bnhf,hf->bnh', xl, a_dst)
            e = jax.nn.leaky_relu(asrc[:, :, None, :] + adst[:, None, :, :], NEG_SLOPE)
            e = jnp.where(mask[..., None], e, NEG_INF)
            attn = jax.nn.softmax(e, axis=1)
            out = jnp.einsum('bsdh,bshf->bdhf', attn, xl)
            if concat:
                out = out.reshape(B, N, H * F)
            else:
                out = out.mean(axis=2)
            return out + bias
        B, N, _ = adj.shape
        mask = (adj > 0) | jnp.eye(N, dtype=bool)[None]
        h = jax.nn.elu(gat_layer(x, mask, W1, att_src1, att_dst1, b1, concat=True))
        h = gat_layer(h, mask, W2, att_src2, att_dst2, b2, concat=False)
        return h
    x = _layernorm(x + _L0_gnn_ref(x, adj, L0_gnn_W, L0_gnn_a), axis=-1)
    x = _layernorm(x + _L1_gnn_ref(adj, x, L1_gnn_W1, L1_gnn_att_src1, L1_gnn_att_dst1, L1_gnn_b1, L1_gnn_W2, L1_gnn_att_src2, L1_gnn_att_dst2, L1_gnn_b2), axis=-1)
    return x

_drawn_inputs = setup_inputs


def setup_inputs(seed=0):
    import zlib

    import numpy as np

    out = dict(_drawn_inputs(seed))
    spreads = {}
    factors = {'L1_gnn_att_dst1': 27.638, 'L1_gnn_att_src2': 6.583, 'L1_gnn_att_dst2': 23.292}
    for name, (base, spread) in spreads.items():
        noise = np.random.default_rng([zlib.crc32(name.encode()), seed]).standard_normal(out[name].shape)
        drawn = base * np.exp(spread * noise) if base else spread * noise
        out[name] = jnp.asarray(drawn.astype(out[name].dtype))
    for name, factor in factors.items():
        out[name] = (out[name] * factor).astype(out[name].dtype)
    return out
```

```python
import concourse.bass as bass
from concourse import mybir
from contextlib import ExitStack

F32 = mybir.dt.float32
F32R = mybir.dt.float32r
BF16 = mybir.dt.bfloat16
I32 = mybir.dt.int32
ALU = mybir.AluOpType
ACT = mybir.ActivationFunctionType

P = 128
SLOPE = 0.2
EPS = 1e-5
BIG = 1e30
DMA = 16


class Layer:

    def __init__(self, name, lag, heads, width, k_tiles, per_chunk):
        self.name = name
        self.lag = lag
        self.H = heads
        self.F = width
        self.KT = k_tiles
        self.G = per_chunk
        self.chunks = [(t, g) for t in range(2) for g in range(heads // per_chunk)]


class Turn:

    def __init__(self, i, counts=None, off=0):
        self.i, self.counts, self.off = i, counts, off
        self.at = i + off

    def batch(self, lag):
        return Turn(self.i, self.counts, self.off - lag)

    def count(self, more, step=1):
        if self.counts is None:
            return (self.at + more) * step
        return self.counts[(self.off + more, step)]


COUNTS = [(k, 1) for k in (-2, -1, 0, 1)]
DMA_COUNTS = [(k, DMA) for k in (-2, -1, 0, 1)]


def gat_kernel(nc, x, adj, w0, a0, w1, asrc1, adst1, b1, w2, asrc2, adst2, b2, out):
    NB, N, D = x.shape
    NT = N // P
    A = Layer("A", 0, 1, D, D // P, 1)
    B = Layer("B", 1, asrc1.shape[0], asrc1.shape[1], D // P, 2)
    C = Layer("C", 2, 1, D, w2.shape[0] // P, 1)
    LAYERS = (A, B, C)
    HD = B.H * B.F

    ctx = ExitStack()
    with ctx:
        def sb(name, shape, dt=F32):
            return ctx.enter_context(nc.sbuf_tensor(name, shape, dt))

        def pb(name, shape, dt=F32):
            return ctx.enter_context(nc.psum_tensor(name, shape, dt))

        def sem(name):
            return ctx.enter_context(nc.semaphore(name))

        ident = sb("ident", [P, P])
        identb = sb("identb", [P, P], BF16)
        ones = sb("ones", [P, P])
        power = sb("power", [P, NT])
        raw0 = sb("raw0", [P, A.KT, D])
        raw1 = sb("raw1", [P, B.KT, HD])
        raw2 = sb("raw2", [P, C.KT, D])
        att0 = sb("att0", [P, 2 * D])
        att1 = sb("att1", [P, 2, HD])
        att2 = sb("att2", [P, 2, D])
        b1p = sb("b1p", [P, HD])
        b2p = sb("b2p", [P, D])
        colsum = sb("colsum", [P, D + 2])
        prod = sb("prod", [P, D])
        minus1 = sb("minus1", [P, 1])
        for L in LAYERS:
            L.W = sb("W" + L.name, [P, L.KT, L.H, L.F + 2])
            L.Wh = sb("Wh" + L.name, [P, L.KT, L.H, L.F + 2], F32R)
            L.Wl = sb("Wl" + L.name, [P, L.KT, L.H, L.F + 2], F32R)

        xin = sb("xin", [P, NT, D])
        adj_in = sb("adj_in", [P, NT, N], I32)
        mask0 = sb("mask0", [P, NT, N], BF16)
        gate0 = sb("gate0", [P, NT, N], BF16)
        fill0 = sb("fill0", [P, NT, N], BF16)
        empty = sb("empty", [P, NT])
        masks = sb("masks", [P, NT, N], BF16)
        gates = sb("gates", [P, NT, N], BF16)
        A.mask = sb("maskA", [P, NT, N], BF16)
        A.gate = gate0
        B.mask = sb("maskB", [P, NT, N], BF16)
        B.gate = sb("gateB", [P, NT, N], BF16)
        C.mask = sb("maskC", [P, NT, N], BF16)
        C.gate = sb("gateC", [P, NT, N], BF16)
        for L in LAYERS:
            n = L.name
            L.inh = sb("inh" + n, [P, L.KT, N], F32R)
            L.inl = sb("inl" + n, [P, L.KT, N], F32R)
            L.V = sb("V" + n, [P, NT, L.H, L.F + 3])
            L.amax = sb("amax" + n, [P, NT, L.H])
            L.top = sb("top" + n, [P, NT, L.H])
            L.lmax = sb("lmax" + n, [P, NT, L.H])
            L.shift = sb("shift" + n, [P, NT, L.H])
            L.a08 = sb("a08" + n, [P, NT, L.H])
            L.a02 = sb("a02" + n, [P, NT, L.H])
            L.prob = [sb(f"prob{n}{h}", [P, NT, N]) for h in range(L.H)]
            L.rden = sb("rden" + n, [P, NT, L.H])
            L.gated = sb("gated" + n, [P, NT, L.H, N], BF16)
            L.stat = sb("stat" + n, [P, NT, 6])
            L.mv = sb("mv" + n, [P, NT, 2])
            L.ve = sb("ve" + n, [P, NT])
            L.nm = sb("nm" + n, [P, NT])
            L.rstd = sb("rstd" + n, [P, NT])
        y0 = sb("y0", [P, NT, D])
        e0 = sb("e0", [P, NT, D])
        x1 = sb("x1", [P, NT, D])
        x1b = sb("x1b", [P, NT, D])
        hid = sb("hid", [P, NT, HD])
        ehid = sb("ehid", [P, NT, HD])
        y2 = sb("y2", [P, NT, D])
        res = sb("res", [P, NT, D])

        TB = [pb(f"TB{i}", [P, 512]) for i in range(2)]
        LB = [pb(f"LB{i}", [P, 512]) for i in range(2)]
        HB = [pb(f"HB{i}", [P, 512]) for i in range(2)]
        AG = [pb(f"AG{i}", [P, 512]) for i in range(2)]
        TBm = TB[0][:, :].bitcast(BF16)

        s_wld, s_cst, s_cst2, s_wab, s_wh, s_wl, s_cs, s_csd, s_b = (sem(n) for n in (
            "weights_loaded", "constants", "identity_made", "score_columns", "w_high", "w_low", "colsum_ready",
            "colsum_kept", "bias_made"))
        s_x, s_adj, s_out = sem("x_loaded"), sem("adj_loaded"), sem("out_stored")
        s_gab, s_mab, s_gbc, s_mbc = sem("gate_a_to_b"), sem("mask_a_to_b"), sem("gate_b_to_c"), sem("mask_b_to_c")
        s_m0, s_m1, s_m1d, s_g0 = sem("mask0_made"), sem("mask1_made"), sem("mask1_diag"), sem("gate0_made")
        s_emp, s_fill, s_mT, s_mA, s_gA = (sem(n) for n in (
            "empty_found", "fill0_made", "masks_transposed", "maskA_made", "gates_made"))
        for L in LAYERS:
            n = L.name
            nin = 2 if L is C else 1
            L.s_inT = [sem(f"inT{u}_{n}") for u in range(nin)]
            L.s_hi = [sem(f"high{u}_{n}") for u in range(nin)]
            L.s_lo = [sem(f"low{u}_{n}") for u in range(nin)]
            L.s_lin = [sem(f"lin{c}_{n}") for c in range(len(L.chunks))]
            L.s_v = [sem(f"values{c}_{n}") for c in range(len(L.chunks))]
            L.s_bca = [sem(f"bc_a{p}_{n}") for p in range(max(1, L.H // 2))]
            L.s_max = [sem(f"max{p}_{n}") for p in range(max(1, L.H // 2))]
            L.s_bias, L.s_top, L.s_lmax, L.s_shift = (sem(k + n) for k in ("bias_", "top_", "lmax_", "shift_"))
            L.s_bcx = [sem(f"bc_bx{h}_{n}") for h in range(L.H)]
            L.s_relu = [sem(f"relu{h}_{n}") for h in range(L.H)]
            L.s_logit = [sem(f"logit{h}_{n}") for h in range(L.H)]
            L.s_exp = [sem(f"exp{h}_{n}") for h in range(L.H)]
            L.s_p = [sem(f"prob{h}_{n}_done") for h in range(L.H)]
            nag = 2 if L.H == 1 else L.H
            L.s_agg = [sem(f"agg{u}_{n}") for u in range(nag)]
            L.s_den = [sem(f"den{u}_{n}") for u in range(nag)]
            L.s_norm = [sem(f"norm{u}_{n}") for u in range(nag)]
        s_fix = sem("scores_fixed_C")
        s_eexp = [sem(f"elu_exp{h}_B") for h in range(B.H)]
        s_elu = [sem(f"elu{h}_B") for h in range(B.H)]
        s_e0, s_y0, s_t0 = sem("elu_exp_A"), sem("elu_A"), sem("residual_A")
        for L in (A, C):
            L.s_st, L.s_mv, L.s_nm, L.s_ve, L.s_rs, L.s_ln = (
                sem(k + L.name) for k in ("stats_", "meanvar_", "negmean_", "vareps_", "rstd_", "normed_"))
        s_x1b = sem("x1b_made")

        USES = {
            "TB0": [(C, C.s_lo[0]), (B, B.s_lo[0]), (A, s_gA)],
            "TB1": [(C, C.s_lo[1]), (A, A.s_lo[0])],
            "LB0": [(C, C.s_v[0]), (B, B.s_v[0]), (B, B.s_v[2]), (A, A.s_v[0])],
            "LB1": [(C, C.s_v[1]), (B, B.s_v[1]), (B, B.s_v[3]), (A, A.s_v[1])],
            "HB0": [(C, C.s_max[0]), (B, B.s_max[1]), (B, B.s_logit[0]), (A, A.s_max[0]), (B, B.s_logit[3])],
            "HB1": [(B, B.s_max[0]), (C, C.s_logit[0]), (B, B.s_logit[1]), (B, B.s_logit[2]), (A, A.s_logit[0])],
            "AG0": [(C, C.s_norm[0]), (B, B.s_norm[0]), (B, B.s_norm[2]), (A, A.s_norm[0])],
            "AG1": [(C, C.s_norm[1]), (B, B.s_norm[1]), (B, B.s_norm[3]), (A, A.s_norm[1])],
        }

        def active(L, i):
            return not isinstance(i.at, int) or 0 <= i.at - L.lag < NB

        def done(eng, s, t, step=1):
            eng.wait_ge(s, t.count(1, step))

        def past(eng, s, t, step=1):
            if not isinstance(t.at, int) or t.at > 0:
                eng.wait_ge(s, t.count(0, step))

        def settle(eng):
            eng.wait_ge(s_cst2, 2)

        def bank_free(eng, bank, s, i):
            uses = USES[bank]
            k = [u[1] is s for u in uses].index(True)
            for back in range(1, 3 * len(uses)):
                L, before = uses[(k - back) % len(uses)]
                t = i.batch((len(uses) - 1 - (k - back)) // len(uses) + L.lag)
                if not isinstance(t.at, int) or 0 <= t.at < NB:
                    eng.wait_ge(before, t.count(1))
                    return

        def iterations(eng, body, needed):
            for i in range(3):
                body(Turn(i))
            regs = {(k, step): eng.alloc_register(f"count{k + 3}x{step}") for k, step in needed}
            with eng.Fori(3, NB - 1) as i:
                counts = {}
                for k, step in needed:
                    r = regs[(k, step)]
                    eng.reg_add(r, i, k)
                    if step > 1:
                        eng.reg_mul(r, r, step)
                    counts[(k, step)] = eng.snap(r, min_val=(3 + k) * step, max_val=(NB + k) * step)
                body(Turn(i, counts))
            for i in range(NB - 1, NB + 2):
                body(Turn(i))

        x_v = x.rearrange("b (n p) f -> b p n f", p=P)
        adj_v = adj.rearrange("b (n p) m -> b p n m", p=P)
        out_v = out.rearrange("b (n p) f -> b p n f", p=P)

        block = ctx.enter_context(nc.Block())

        @block.sync
        def _(sp):
            sp.dma_start(raw0[:, :, :], w0.rearrange("(k p) f -> p k f", p=P)).then_inc(s_wld, DMA)
            sp.dma_start(raw1[:, :, :], w1.rearrange("(k p) f -> p k f", p=P)).then_inc(s_wld, DMA)
            sp.dma_start(raw2[:, :, :], w2.rearrange("(k p) f -> p k f", p=P)).then_inc(s_wld, DMA)

            def everywhere(v):
                return v.partition_broadcast(P)

            sp.dma_start(att0[:, :], everywhere(a0.rearrange("f o -> (f o)"))).then_inc(s_wld, DMA)
            sp.dma_start(att1[:, 0, :], everywhere(asrc1.rearrange("h f -> (h f)"))).then_inc(s_wld, DMA)
            sp.dma_start(att1[:, 1, :], everywhere(adst1.rearrange("h f -> (h f)"))).then_inc(s_wld, DMA)
            sp.dma_start(att2[:, 0, :], everywhere(asrc2.rearrange("h f -> (h f)"))).then_inc(s_wld, DMA)
            sp.dma_start(att2[:, 1, :], everywhere(adst2.rearrange("h f -> (h f)"))).then_inc(s_wld, DMA)
            sp.dma_start(b1p[:, :], everywhere(b1)).then_inc(s_wld, DMA)
            sp.dma_start(b2p[:, :], everywhere(b2)).then_inc(s_wld, DMA)
            sp.dma_start(xin[:, :, :], x_v[0]).then_inc(s_x, DMA)
            sp.dma_start(adj_in[:, :, :], adj_v[0]).then_inc(s_adj, DMA)

            def body(i):
                tA, tB, tC = i.batch(A.lag), i.batch(B.lag), i.batch(C.lag)
                if active(B, i):
                    done(sp, s_gab, tB, DMA)
                    past(sp, C.s_max[0], tB)
                    sp.dma_start(C.gate[:, :, :], B.gate[:, :, :]).then_inc(s_gbc, DMA)
                if active(A, i) and not (isinstance(i.at, int) and i.at == NB - 1):
                    done(sp, s_m0, tA)
                    done(sp, s_m1, tA)
                    sp.dma_start(adj_in[:, :, :], adj_v[i.at + 1]).then_inc(s_adj, DMA)
                if active(B, i):
                    done(sp, s_mab, tB, DMA)
                    past(sp, C.s_p[0], tB)
                    sp.dma_start(C.mask[:, :, :], B.mask[:, :, :]).then_inc(s_mbc, DMA)
                if active(A, i):
                    done(sp, s_m1d, tA)
                    past(sp, B.s_p[B.H - 1], tA)
                    past(sp, s_mbc, tA, DMA)
                    sp.dma_start(B.mask[:, :, :], masks[:, :, :]).then_inc(s_mab, DMA)
                if active(C, i):
                    done(sp, C.s_ln, tC)
                    sp.dma_start(out_v[tC.at], res[:, :, :]).then_inc(s_out, DMA)
                if active(A, i):
                    done(sp, s_gA, tA)
                    past(sp, B.s_max[1], tA)
                    past(sp, s_gbc, tA, DMA)
                    sp.dma_start(B.gate[:, :, :], gates[:, :, :]).then_inc(s_gab, DMA)
                if active(A, i) and not (isinstance(i.at, int) and i.at == NB - 1):
                    done(sp, A.s_inT[0], tA)
                    done(sp, s_t0, tA)
                    sp.dma_start(xin[:, :, :], x_v[i.at + 1]).then_inc(s_x, DMA)

            iterations(sp, body, COUNTS + DMA_COUNTS)
            sp.wait_ge(s_out, DMA * NB)

        @block.gpsimd
        def _(pool):
            pool.memset(ident[:, :], 0.0).then_inc(s_cst, 1)
            pool.memset(identb[:, :], 0.0).then_inc(s_cst, 1)
            pool.memset(ones[:, :], 1.0).then_inc(s_cst, 1)
            pool.memset(power[:, :], -0.5).then_inc(s_cst, 1)
            for L in LAYERS:
                pool.memset(L.V[:, :, :, L.F + 2], 1.0).then_inc(s_cst, 1)
            pool.wait_ge(s_cst, 7)
            for m in (ident, identb):
                pool.affine_select(out=m[:, :], in_=m[:, :], compare_op=ALU.not_equal, fill=1.0, base=0,
                                   pattern=[[-1, P]], channel_multiplier=1).then_inc(s_cst2, 1)
            pool.wait_ge(s_b, 2)

            def biases(L, t):
                settle(pool)
                if L is C:
                    done(pool, s_fix, t)
                for s in L.s_v:
                    done(pool, s, t)
                past(pool, L.s_relu[-1], t)
                pool.tensor_scalar(L.a08[:, :, :], L.V[:, :, :, 0], 1.0 - SLOPE, 1.0, ALU.mult, ALU.mult)
                settle(pool)
                past(pool, L.s_exp[-1], t)
                pool.tensor_scalar(L.a02[:, :, :], L.V[:, :, :, 0], SLOPE, 1.0, ALU.mult, ALU.mult)\
                    .then_inc(L.s_bias, 1)

            def norm(L, t, src, dst):
                settle(pool)
                done(pool, L.s_mv, t)
                pool.tensor_scalar(L.nm[:, :], L.mv[:, :, 0], -1.0, 1.0, ALU.mult, ALU.mult).then_inc(L.s_nm, 1)
                pool.tensor_scalar(L.ve[:, :], L.mv[:, :, 1], 1.0, EPS, ALU.mult, ALU.add).then_inc(L.s_ve, 1)
                done(pool, L.s_ve, t)
                pool.tensor_tensor(L.rstd[:, :], L.ve[:, :], power[:, :], ALU.pow).then_inc(L.s_rs, 1)
                settle(pool)
                done(pool, L.s_nm, t)
                done(pool, L.s_rs, t)
                for k in range(NT):
                    last = pool.tensor_scalar(dst[:, k, :], src[:, k, :], L.nm[:, k:k + 1], L.rstd[:, k:k + 1],
                                              ALU.add, ALU.mult)
                last.then_inc(L.s_ln, 1)

            def body(i):
                tA, tB, tC = i.batch(A.lag), i.batch(B.lag), i.batch(C.lag)
                if active(C, i):
                    biases(C, tC)
                if active(B, i):
                    biases(B, tB)
                if active(A, i):
                    settle(pool)
                    done(pool, s_m0, tA)
                    past(pool, A.s_max[0], tA)
                    pool.tensor_scalar(gate0[:, :, :], mask0[:, :, :], -1.0, BIG, ALU.add, ALU.mult).then_inc(s_g0, 1)
                    settle(pool)
                    done(pool, s_m1, tA)
                    for k in range(NT):
                        d = masks[:, k, k * P:(k + 1) * P]
                        last = pool.affine_select(out=d, in_=d, compare_op=ALU.not_equal, fill=1.0, base=0,
                                                  pattern=[[-1, P]], channel_multiplier=1)
                    last.then_inc(s_m1d, 1)
                    biases(A, tA)
                if active(C, i):
                    settle(pool)
                    past(pool, s_out, tC, DMA)
                    norm(C, tC, y2, res)
                if active(B, i):
                    done(pool, A.s_ln, tB)
                    past(pool, C.s_norm[1], tB)
                    pool.tensor_tensor(x1b[:, :, :], x1[:, :, :], b2p[:, :].unsqueeze(1).to_broadcast([P, NT, D]),
                                       ALU.add).then_inc(s_x1b, 1)
                if active(A, i):
                    done(pool, s_y0, tA)
                    done(pool, s_x, tA, DMA)
                    pool.tensor_tensor(y0[:, :, :], y0[:, :, :], xin[:, :, :], ALU.add).then_inc(s_t0, 1)
                    settle(pool)
                    past(pool, B.s_inT[0], tA)
                    past(pool, s_x1b, tA)
                    norm(A, tA, y0, x1)

            iterations(pool, body, COUNTS + DMA_COUNTS)

        @block.scalar
        def _(act):
            def high(L, u, bank, t):
                done(act, L.s_inT[u], t)
                past(act, L.s_lin[-1], t)
                nc.scalar.activation(L.inh[:, 2 * u:2 * u + 2, :], bank[:, :].rearrange("p (k n) -> p k n", k=2),
                                     ACT.Copy).then_inc(L.s_hi[u], 1)

            def values(L, c, bank, t):
                tile, g = L.chunks[c]
                done(act, L.s_lin[c], t)
                past(act, L.s_agg[-1], t)
                past(act, L.s_shift, t)
                past(act, L.s_bias, t)
                w = L.G * (L.F + 2)
                nc.scalar.activation(L.V[:, tile, g * L.G:(g + 1) * L.G, 0:L.F + 2],
                                     bank[:, 0:w].rearrange("p (h f) -> p h f", h=L.G), ACT.Copy)\
                    .then_inc(L.s_v[c], 1)

            def relu(L, h, bank, t):
                done(act, L.s_bcx[h], t)
                done(act, L.s_bias, t)
                past(act, L.s_agg[h if L.H > 1 else -1], t)
                for k in range(NT):
                    last = nc.scalar.activation(L.prob[h][:, k, :], bank[:, 0:N], ACT.Relu,
                                                bias=L.a08[:, k, h:h + 1], scale=1.0 - SLOPE)
                last.then_inc(L.s_relu[h], 1)

            def exp(L, h, t):
                done(act, L.s_logit[h], t)
                for k in range(NT):
                    last = nc.scalar.activation(L.prob[h][:, k, :], L.prob[h][:, k, :], ACT.Exp,
                                                bias=L.a02[:, k, h:h + 1])
                last.then_inc(L.s_exp[h], 1)

            def elu_exp(h, t):
                done(act, B.s_norm[h], t)
                s = slice(h * B.F, (h + 1) * B.F)
                nc.scalar.activation(ehid[:, :, s], hid[:, :, s], ACT.Exp, bias=minus1[:, :]).then_inc(s_eexp[h], 1)


            act.wait_ge(s_b, 3)

            def body(i):
                tA, tB, tC = i.batch(A.lag), i.batch(B.lag), i.batch(C.lag)
                a, b, c = active(A, i), active(B, i), active(C, i)
                if c:
                    high(C, 0, TB[0], tC)
                    high(C, 1, TB[1], tC)
                if b:
                    high(B, 0, TB[0], tB)
                if c:
                    values(C, 0, LB[0], tC)
                    values(C, 1, LB[1], tC)
                if b:
                    for k in range(4):
                        values(B, k, LB[k % 2], tB)
                if a:
                    high(A, 0, TB[1], tA)
                    values(A, 0, LB[0], tA)
                    values(A, 1, LB[1], tA)
                if c:
                    relu(C, 0, HB[1], tC)
                if b:
                    relu(B, 0, HB[0], tB)
                if c:
                    exp(C, 0, tC)
                if b:
                    relu(B, 1, HB[1], tB)
                    exp(B, 0, tB)
                    exp(B, 1, tB)
                    relu(B, 2, HB[1], tB)
                    elu_exp(0, tB)
                    relu(B, 3, HB[0], tB)
                    exp(B, 2, tB)
                if a:
                    relu(A, 0, HB[1], tA)
                if b:
                    exp(B, 3, tB)
                    elu_exp(1, tB)
                if a:
                    exp(A, 0, tA)
                if b:
                    elu_exp(2, tB)
                    elu_exp(3, tB)
                if a:
                    done(act, A.s_norm[0], tA)
                    done(act, A.s_norm[1], tA)
                    nc.scalar.activation(e0[:, :, :], y0[:, :, :], ACT.Exp, bias=minus1[:, :]).then_inc(s_e0, 1)

            iterations(act, body, COUNTS)

        @block.vector
        def _(dve):
            dve.wait_ge(s_wld, DMA * 10)
            n_ab = 0
            for k in range(A.KT):
                for j in range(2):
                    nc.vector.scalar_tensor_tensor(out=prod[:, :], in0=raw0[:, k, :], scalar=1.0,
                                                   in1=att0[:, (1 - j) * D:(2 - j) * D], op0=ALU.mult, op1=ALU.mult,
                                                   accum_out=A.W[:, k, 0, j:j + 1]).then_inc(s_wab, 1)
                    n_ab += 1
                    dve.wait_ge(s_wab, n_ab)
            for k in range(B.KT):
                for h in range(B.H):
                    for j in range(2):
                        s = slice(h * B.F, (h + 1) * B.F)
                        nc.vector.scalar_tensor_tensor(out=prod[:, 0:B.F], in0=raw1[:, k, s], scalar=1.0,
                                                       in1=att1[:, j, s], op0=ALU.mult, op1=ALU.mult,
                                                       accum_out=B.W[:, k, h, j:j + 1]).then_inc(s_wab, 1)
                        n_ab += 1
                        dve.wait_ge(s_wab, n_ab)
            for k in range(C.KT):
                for j in range(2):
                    nc.vector.scalar_tensor_tensor(out=prod[:, :], in0=raw2[:, k, :], scalar=1.0, in1=att2[:, j, :],
                                                   op0=ALU.mult, op1=ALU.mult,
                                                   accum_out=C.W[:, k, 0, j:j + 1]).then_inc(s_wab, 1)
                    n_ab += 1
                    dve.wait_ge(s_wab, n_ab)
            for k in range(A.KT):
                nc.vector.tensor_copy(A.W[:, k, 0, 2:D + 2], raw0[:, k, :]).then_inc(s_wab, 1)
            for k in range(B.KT):
                nc.vector.tensor_copy(B.W[:, k, :, 2:B.F + 2], raw1[:, k, :].rearrange("p (h f) -> p h f", h=B.H))\
                    .then_inc(s_wab, 1)
            for k in range(C.KT):
                nc.vector.tensor_copy(C.W[:, k, 0, 2:D + 2], raw2[:, k, :]).then_inc(s_wab, 1)
            n_ab += A.KT + B.KT + C.KT
            dve.wait_ge(s_wab, n_ab)
            for L in LAYERS:
                nc.vector.tensor_copy(L.Wh[:, :, :, :], L.W[:, :, :, :]).then_inc(s_wh, 1)
            dve.wait_ge(s_wh, 3)
            for L in LAYERS:
                nc.vector.tensor_tensor(L.Wl[:, :, :, :], L.W[:, :, :, :], L.Wh[:, :, :, :].bitcast(F32),
                                        ALU.subtract).then_inc(s_wl, 1)
            dve.wait_ge(s_cs, 1)
            nc.vector.tensor_copy(colsum[:, :], AG[0][:, 0:D + 2]).then_inc(s_csd, 1)
            dve.wait_ge(s_csd, 1)
            nc.vector.tensor_tensor(b2p[:, :], b2p[:, :], colsum[:, 2:D + 2], ALU.subtract).then_inc(s_b, 1)
            nc.vector.tensor_scalar(b1p[:, :], b1p[:, :], 1.0, None, ALU.add).then_inc(s_b, 1)
            nc.vector.memset(minus1[:, :], -1.0).then_inc(s_b, 1)
            dve.wait_ge(s_b, 3)

            def low(L, u, bank, t):
                done(dve, L.s_hi[u], t)
                past(dve, L.s_lin[-1], t)
                nc.vector.tensor_tensor(L.inl[:, 2 * u:2 * u + 2, :], bank[:, :].rearrange("p (k n) -> p k n", k=2),
                                        L.inh[:, 2 * u:2 * u + 2, :].bitcast(F32), ALU.subtract).then_inc(L.s_lo[u], 1)

            def maxima(L, p, bank, t):
                settle(dve)
                done(dve, L.s_bca[p], t)
                if L is not A and p == 0:
                    done(dve, s_gab if L is B else s_gbc, t, DMA)
                heads = range(2 * p, min(2 * p + 2, L.H))
                for h in heads:
                    for k in range(NT):
                        last = nc.vector.tensor_tensor_reduce(
                            out=L.gated[:, k, h, :], in0=bank[:, (h - 2 * p) * N:(h - 2 * p + 1) * N], in1=L.gate[:, k, :],
                            scale=1.0, scalar=-3e38, op0=ALU.add, op1=ALU.max, accum_out=L.amax[:, k, h:h + 1])
                last.then_inc(L.s_max[p], 1)

            def shifts(L, t):
                for s in L.s_max:
                    done(dve, s, t)
                nc.vector.tensor_tensor(L.top[:, :, :], L.amax[:, :, :], L.V[:, :, :, 1], ALU.add).then_inc(L.s_top, 1)
                done(dve, L.s_top, t)
                nc.vector.scalar_tensor_tensor(out=L.lmax[:, :, :], in0=L.top[:, :, :], scalar=SLOPE, in1=L.top[:, :, :],
                                               op0=ALU.mult, op1=ALU.max).then_inc(L.s_lmax, 1)
                done(dve, L.s_lmax, t)
                past(dve, L.s_bcx[-1], t)
                nc.vector.scalar_tensor_tensor(out=L.shift[:, :, :], in0=L.V[:, :, :, 1], scalar=SLOPE,
                                               in1=L.lmax[:, :, :], op0=ALU.mult, op1=ALU.subtract).then_inc(L.s_shift, 1)

            def logit(L, h, bank, t):
                done(dve, L.s_relu[h], t)
                nc.vector.tensor_tensor(L.prob[h][:, :, :], L.prob[h][:, :, :],
                                        bank[:, N:2 * N].unsqueeze(1).to_broadcast([P, NT, N]), ALU.add)\
                    .then_inc(L.s_logit[h], 1)

            def masked(L, h, t):
                done(dve, L.s_exp[h], t)
                nc.vector.tensor_tensor(L.prob[h][:, :, :], L.prob[h][:, :, :], L.mask[:, :, :], ALU.min)\
                    .then_inc(L.s_p[h], 1)

            def norm_head(h, bank, t):
                done(dve, B.s_agg[h], t)
                S = B.F + 1
                nc.vector.reciprocal(B.rden[:, :, h], bank[:, 0:2 * S].rearrange("p (k s) -> p k s", s=S)[:, :, B.F])\
                    .then_inc(B.s_den[h], 1)
                done(dve, B.s_den[h], t)
                for u in C.s_inT:
                    past(dve, u, t)
                for k in range(NT):
                    last = nc.vector.scalar_tensor_tensor(
                        out=hid[:, k, h * B.F:(h + 1) * B.F], in0=bank[:, k * S:k * S + B.F],
                        scalar=B.rden[:, k, h:h + 1], in1=b1p[:, h * B.F:(h + 1) * B.F], op0=ALU.mult, op1=ALU.add)
                last.then_inc(B.s_norm[h], 1)

            def elu_head(h, t):
                done(dve, s_eexp[h], t)
                s = slice(h * B.F, (h + 1) * B.F)
                nc.vector.scalar_tensor_tensor(out=hid[:, :, s], in0=ehid[:, :, s], scalar=1.0, in1=hid[:, :, s],
                                               op0=ALU.min, op1=ALU.max).then_inc(s_elu[h], 1)

            def norm_tile(L, k, bank, t):
                done(dve, L.s_agg[k], t)
                nc.vector.reciprocal(L.rden[:, k, :], bank[:, L.F:L.F + 1]).then_inc(L.s_den[k], 1)
                done(dve, L.s_den[k], t)
                if L is A:
                    past(dve, A.s_ln, t)
                    nc.vector.tensor_scalar(y0[:, k, :], bank[:, 0:D], L.rden[:, k, :], 1.0, ALU.mult, ALU.add)\
                        .then_inc(L.s_norm[k], 1)
                else:
                    past(dve, C.s_ln, t)
                    done(dve, s_x1b, t)
                    nc.vector.scalar_tensor_tensor(out=y2[:, k, :], in0=bank[:, 0:D], scalar=L.rden[:, k, :],
                                                   in1=x1b[:, k, :], op0=ALU.mult, op1=ALU.add).then_inc(L.s_norm[k], 1)

            def stats(L, src, t):
                past(dve, L.s_ln, t)
                for k in range(NT):
                    last = nc.vector.bn_stats(L.stat[:, k, :], src[:, k, :])
                last.then_inc(L.s_st, 1)
                settle(dve)
                done(dve, L.s_st, t)
                for k in range(NT):
                    last = nc.vector.bn_aggr(L.mv[:, k, :], L.stat[:, k, :])
                last.then_inc(L.s_mv, 1)

            def body(i):
                tA, tB, tC = i.batch(A.lag), i.batch(B.lag), i.batch(C.lag)
                a, b, c = active(A, i), active(B, i), active(C, i)
                if c:
                    low(C, 0, TB[0], tC)
                    low(C, 1, TB[1], tC)
                if b:
                    low(B, 0, TB[0], tB)
                if a:
                    done(dve, s_adj, tA, DMA)
                    past(dve, s_fill, tA)
                    past(dve, s_g0, tA)
                    nc.vector.tensor_scalar(mask0[:, :, :], adj_in[:, :, :], 0, None, ALU.not_equal).then_inc(s_m0, 1)
                    past(dve, s_mab, tA, DMA)
                    past(dve, s_mT, tA)
                    nc.vector.tensor_scalar(masks[:, :, :], adj_in[:, :, :], 0, None, ALU.is_gt).then_inc(s_m1, 1)
                if c:
                    done(dve, C.s_v[0], tC)
                    done(dve, C.s_v[1], tC)
                    nc.vector.tensor_tensor(C.V[:, :, 0, 0:2], C.V[:, :, 0, 0:2],
                                            colsum[:, 0:2].unsqueeze(1).to_broadcast([P, NT, 2]), ALU.subtract)\
                        .then_inc(s_fix, 1)
                    maxima(C, 0, HB[0], tC)
                    shifts(C, tC)
                if b:
                    maxima(B, 0, HB[1], tB)
                    maxima(B, 1, HB[0], tB)
                    for s in B.s_v:
                        done(dve, s, tB)
                    shifts(B, tB)
                if a:
                    low(A, 0, TB[1], tA)
                if c:
                    logit(C, 0, HB[1], tC)
                if b:
                    logit(B, 0, HB[0], tB)
                if c:
                    done(dve, s_mbc, tC, DMA)
                    masked(C, 0, tC)
                if b:
                    logit(B, 1, HB[1], tB)
                    done(dve, s_mab, tB, DMA)
                    masked(B, 0, tB)
                if a:
                    settle(dve)
                    done(dve, s_g0, tA)
                    maxima(A, 0, HB[0], tA)
                    for s in A.s_v:
                        done(dve, s, tA)
                    shifts(A, tA)
                    past(dve, s_fill, tA)
                    nc.vector.tensor_scalar(empty[:, :], A.amax[:, :, 0], -0.5 * BIG, None, ALU.is_lt).then_inc(s_emp, 1)
                    done(dve, s_emp, tA)
                    past(dve, s_mT, tA)
                    for k in range(NT):
                        last = nc.vector.tensor_scalar(fill0[:, k, :], mask0[:, k, :], empty[:, k:k + 1], None, ALU.max)
                    last.then_inc(s_fill, 1)
                if b:
                    masked(B, 1, tB)
                if c:
                    norm_tile(C, 0, AG[0], tC)
                    norm_tile(C, 1, AG[1], tC)
                if b:
                    logit(B, 2, HB[1], tB)
                    norm_head(0, AG[0], tB)
                    logit(B, 3, HB[0], tB)
                    norm_head(1, AG[1], tB)
                    masked(B, 2, tB)
                if c:
                    for s in C.s_norm:
                        done(dve, s, tC)
                    stats(C, y2, tC)
                if a:
                    logit(A, 0, HB[1], tA)
                    done(dve, s_mT, tA)
                    past(dve, A.s_p[0], tA)
                    nc.vector.tensor_copy(A.mask[:, :, :], TBm[:, 0:NT * N].rearrange("p (k n) -> p k n", k=NT))\
                        .then_inc(s_mA, 1)
                    past(dve, s_gab, tA, DMA)
                    nc.vector.tensor_scalar(gates[:, :, :], TBm[:, NT * N:2 * NT * N].rearrange("p (k n) -> p k n", k=NT),
                                            -1.0, BIG, ALU.add, ALU.mult).then_inc(s_gA, 1)
                if b:
                    masked(B, 3, tB)
                    elu_head(0, tB)
                if a:
                    done(dve, s_mA, tA)
                    masked(A, 0, tA)
                if b:
                    norm_head(2, AG[0], tB)
                    elu_head(1, tB)
                    norm_head(3, AG[1], tB)
                    elu_head(2, tB)
                    elu_head(3, tB)
                if a:
                    norm_tile(A, 0, AG[0], tA)
                    norm_tile(A, 1, AG[1], tA)
                    done(dve, s_e0, tA)
                    nc.vector.scalar_tensor_tensor(out=y0[:, :, :], in0=e0[:, :, :], scalar=1.0, in1=y0[:, :, :],
                                                   op0=ALU.min, op1=ALU.max).then_inc(s_y0, 1)
                    done(dve, s_t0, tA)
                    stats(A, y0, tA)

            iterations(dve, body, COUNTS + DMA_COUNTS)

        @block.tensor
        def _(pe):
            pe.wait_ge(s_cst, 7)
            pe.wait_ge(s_cst2, 2)
            pe.wait_ge(s_wl, 3)
            for k in range(C.KT):
                last = nc.tensor.matmul(AG[0][:, 0:D + 2], ones[:, :], C.W[:, k, 0, :], start=(k == 0), stop=(k == C.KT - 1))
            last.then_inc(s_cs, 1)
            pe.wait_ge(s_csd, 1)

            def turn(bank, k, n, src):
                return nc.tensor.transpose(bank[:, k * N + n * P:k * N + (n + 1) * P], src, ident[:, :])

            def project(L, c, bank, t):
                tile, g = L.chunks[c]
                for s in L.s_lo:
                    done(pe, s, t)
                w = L.G * (L.F + 2)
                terms = [(x_, w_, k) for k in range(L.KT) for x_, w_ in ((L.inh, L.Wh), (L.inh, L.Wl), (L.inl, L.Wh))]
                for n, (x_, w_, k) in enumerate(terms):
                    last = nc.tensor.matmul(bank[:, 0:w], x_[:, k, tile * P:(tile + 1) * P],
                                            w_[:, k, g * L.G:(g + 1) * L.G, :].rearrange("p h f -> p (h f)"),
                                            start=(n == 0), stop=(n == len(terms) - 1))
                last.then_inc(L.s_lin[c], 1)

            def spread(bank, off, column):
                return nc.tensor.transpose(bank[:, off:off + P], column.to_broadcast([P, P]), ident[:, :])

            def bc_a(L, p, bank, t):
                for s in L.s_v:
                    done(pe, s, t)
                for h in range(2 * p, min(2 * p + 2, L.H)):
                    for k in range(NT):
                        last = spread(bank, (h - 2 * p) * N + k * P, L.V[:, k, h, 0:1])
                last.then_inc(L.s_bca[p], 1)

            def bc_bx(L, h, bank, t):
                done(pe, L.s_shift, t)
                for k in range(NT):
                    spread(bank, k * P, L.V[:, k, h, 1:2])
                    last = spread(bank, N + k * P, L.shift[:, k, h:h + 1])
                last.then_inc(L.s_bcx[h], 1)

            def weigh(L, h, d, bank, off):
                for k in range(NT):
                    last = nc.tensor.matmul(bank[:, off:off + L.F + 1], L.prob[h][:, k, d * P:(d + 1) * P],
                                            L.V[:, k, h, 2:L.F + 3], start=(k == 0), stop=(k == NT - 1))
                return last

            def agg_tile(L, d, bank, t):
                done(pe, L.s_p[0], t)
                weigh(L, 0, d, bank, 0).then_inc(L.s_agg[d], 1)

            def agg_head(h, bank, t):
                done(pe, B.s_p[h], t)
                for d in range(NT):
                    last = weigh(B, h, d, bank, d * (B.F + 1))
                last.then_inc(B.s_agg[h], 1)

            def body(i):
                tA, tB, tC = i.batch(A.lag), i.batch(B.lag), i.batch(C.lag)
                a, b, c = active(A, i), active(B, i), active(C, i)
                if c:
                    for s in s_elu:
                        done(pe, s, tC)
                    for u in range(2):
                        bank_free(pe, f"TB{u}", C.s_lo[u], i)
                        for k in range(2):
                            for n in range(NT):
                                last = turn(TB[u], k, n, hid[:, n, (2 * u + k) * P:(2 * u + k + 1) * P])
                        last.then_inc(C.s_inT[u], 1)
                if b:
                    bank_free(pe, "TB0", B.s_lo[0], i)
                    done(pe, A.s_ln, tB)
                    for k in range(2):
                        for n in range(NT):
                            last = turn(TB[0], k, n, x1[:, n, k * P:(k + 1) * P])
                    last.then_inc(B.s_inT[0], 1)
                if c:
                    for k in range(2):
                        bank_free(pe, f"LB{k}", C.s_v[k], i)
                        project(C, k, LB[k], tC)
                if b:
                    for k in range(4):
                        bank_free(pe, f"LB{k % 2}", B.s_v[k], i)
                        project(B, k, LB[k % 2], tB)
                if c:
                    bank_free(pe, "HB0", C.s_max[0], i)
                    done(pe, s_fix, tC)
                    bc_a(C, 0, HB[0], tC)
                if b:
                    bank_free(pe, "HB1", B.s_max[0], i)
                    bc_a(B, 0, HB[1], tB)
                    bank_free(pe, "HB0", B.s_max[1], i)
                    bc_a(B, 1, HB[0], tB)
                if a:
                    bank_free(pe, "TB1", A.s_lo[0], i)
                    done(pe, s_x, tA, DMA)
                    for k in range(2):
                        for n in range(NT):
                            last = turn(TB[1], k, n, xin[:, n, k * P:(k + 1) * P])
                    last.then_inc(A.s_inT[0], 1)
                    for k in range(2):
                        bank_free(pe, f"LB{k}", A.s_v[k], i)
                        project(A, k, LB[k], tA)
                if c:
                    bank_free(pe, "HB1", C.s_logit[0], i)
                    bc_bx(C, 0, HB[1], tC)
                if b:
                    bank_free(pe, "HB0", B.s_logit[0], i)
                    bc_bx(B, 0, HB[0], tB)
                    bank_free(pe, "HB1", B.s_logit[1], i)
                    bc_bx(B, 1, HB[1], tB)
                if a:
                    bank_free(pe, "HB0", A.s_max[0], i)
                    bc_a(A, 0, HB[0], tA)
                if c:
                    for k in range(NT):
                        bank_free(pe, f"AG{k}", C.s_norm[k], i)
                        agg_tile(C, k, AG[k], tC)
                if b:
                    bank_free(pe, "HB1", B.s_logit[2], i)
                    bc_bx(B, 2, HB[1], tB)
                    bank_free(pe, "AG0", B.s_norm[0], i)
                    agg_head(0, AG[0], tB)
                    bank_free(pe, "HB0", B.s_logit[3], i)
                    bc_bx(B, 3, HB[0], tB)
                    bank_free(pe, "AG1", B.s_norm[1], i)
                    agg_head(1, AG[1], tB)
                if a:
                    bank_free(pe, "TB0", s_gA, i)
                    done(pe, s_fill, tA)
                    done(pe, s_m1d, tA)
                    for n, m in enumerate((fill0, masks)):
                        for k in range(NT):
                            for q in range(NT):
                                o = (n * NT + k) * N + q * P
                                last = nc.tensor.transpose(TBm[:, o:o + P], m[:, q, k * P:(k + 1) * P], identb[:, :])
                    last.then_inc(s_mT, 1)
                    bank_free(pe, "HB1", A.s_logit[0], i)
                    bc_bx(A, 0, HB[1], tA)
                if b:
                    bank_free(pe, "AG0", B.s_norm[2], i)
                    agg_head(2, AG[0], tB)
                    bank_free(pe, "AG1", B.s_norm[3], i)
                    agg_head(3, AG[1], tB)
                if a:
                    for k in range(NT):
                        bank_free(pe, f"AG{k}", A.s_norm[k], i)
                        agg_tile(A, k, AG[k], tA)

            iterations(pe, body, COUNTS + DMA_COUNTS)


_INS = ["x", "adj", "L0_gnn_W", "L0_gnn_a", "L1_gnn_W1", "L1_gnn_att_src1", "L1_gnn_att_dst1", "L1_gnn_b1",
        "L1_gnn_W2", "L1_gnn_att_src2", "L1_gnn_att_dst2", "L1_gnn_b2"]


def kernel(**inputs):
    import numpy as _np
    import concourse.bacc as _bacc
    from concourse import mybir as _mybir
    from concourse.bass_utils import run_bass_kernel_spmd as _run

    nc = _bacc.Bacc("TRN2", target_bir_lowering=False, num_devices=1)
    arrays, args = {}, []
    for name in _INS:
        a = _np.ascontiguousarray(inputs[name])
        arrays[f"in_{name}_dram"] = a
        args.append(nc.dram_tensor(f"in_{name}_dram", a.shape, _mybir.dt.from_np(a.dtype), kind="ExternalInput").ap())
    out = nc.dram_tensor("out_0_dram", inputs["x"].shape, F32, kind="ExternalOutput").ap()
    gat_kernel(nc, *args, out)
    r = _run(nc, [arrays], core_ids=[0])
    return r.results[0]["out_0_dram"]
```

```python
import concourse.bass as bass
from concourse import mybir
from contextlib import ExitStack

F32 = mybir.dt.float32
F32R = mybir.dt.float32r
BF16 = mybir.dt.bfloat16
I32 = mybir.dt.int32
ALU = mybir.AluOpType
ACT = mybir.ActivationFunctionType

P = 128
SLOPE = 0.2
EPS = 1e-5
BIG = 2.0 ** 100
DMA = 16


class Layer:

    def __init__(self, name, heads, width, k_tiles, per_chunk):
        self.name = name
        self.H = heads
        self.F = width
        self.KT = k_tiles
        self.G = per_chunk
        self.chunks = [(t, g) for t in range(2) for g in range(heads // per_chunk)]


class Turn:

    def __init__(self, i, counts=None, off=0):
        self.i, self.counts, self.off = i, counts, off
        self.at = i + off

    def batch(self, lag):
        return Turn(self.i, self.counts, self.off - lag)

    def this(self, step=1):
        return (self.at + 1) * step if self.counts is None else self.counts[(self.off + 1, step)]

    def last(self, step=1):
        return self.at * step if self.counts is None else self.counts[(self.off, step)]

    @property
    def later(self):
        return self.counts is not None or self.at > 0


COUNTS = [(k, 1) for k in range(-4, 2)]
DMA_COUNTS = [(k, DMA) for k in range(-4, 2)]


def gat_kernel(nc, x, adj, w0, a0, w1, asrc1, adst1, b1, w2, asrc2, adst2, b2, out):
    NB, N, D = x.shape
    NT = N // P
    A = Layer("A", 1, D, D // P, 1)
    B = Layer("B", asrc1.shape[0], asrc1.shape[1], D // P, 2)
    C = Layer("C", 1, D, w2.shape[0] // P, 1)
    LAYERS = (A, B, C)
    B.prepared, C.prepared = 0, 0
    HD = B.H * B.F

    ctx = ExitStack()
    with ctx:
        def sb(name, shape, dt=F32):
            return ctx.enter_context(nc.sbuf_tensor(name, shape, dt))

        def pb(name, shape, dt=F32):
            return ctx.enter_context(nc.psum_tensor(name, shape, dt))

        def sem(name):
            return ctx.enter_context(nc.semaphore(name))

        ident = sb("ident", [P, P])
        identb = sb("identb", [P, P], BF16)
        ones = sb("ones", [P, P])
        power = sb("power", [P, NT])
        raw0 = sb("raw0", [P, A.KT, D])
        raw1 = sb("raw1", [P, B.KT, HD])
        raw2 = sb("raw2", [P, C.KT, D])
        att0 = sb("att0", [P, 2 * D])
        att1 = sb("att1", [P, 2, HD])
        att2 = sb("att2", [P, 2, D])
        b1p = sb("b1p", [P, HD])
        b2p = sb("b2p", [P, D])
        colsum = sb("colsum", [P, D + 2])
        prod = sb("prod", [P, 2, D])
        minus1 = sb("minus1", [P, 1])
        for L in LAYERS:
            L.W = sb("W" + L.name, [P, L.KT, L.H, L.F + 2])
            L.Wh = sb("Wh" + L.name, [P, L.KT, L.H, L.F + 2], F32R)
            L.Wl = sb("Wl" + L.name, [P, L.KT, L.H, L.F + 2], F32R)

        xin = sb("xin", [P, NT, D])
        xres = sb("xres", [P, NT, D])
        adj_in = sb("adj_in", [P, NT, N], I32)
        A.gate = sb("gateA", [P, NT, N], BF16)
        masks = sb("masks", [P, NT, N], BF16)
        gates = sb("gates", [P, NT, N], BF16)
        B.gate = sb("gateB", [P, NT, N], BF16)
        C.gate = sb("gateC", [P, NT, N], BF16)
        for L in LAYERS:
            n = L.name
            L.inh = sb("inh" + n, [P, L.KT, N], F32R)
            L.inl = sb("inl" + n, [P, L.KT, N], F32R)
            L.V = sb("V" + n, [P, NT, L.H, L.F + 3])
            L.amax = sb("amax" + n, [P, NT, L.H])
            L.top = sb("top" + n, [P, NT, L.H])
            L.lmax = sb("lmax" + n, [P, NT, L.H])
            L.shift = sb("shift" + n, [P, NT, L.H])
            L.b4 = sb("b4" + n, [P, NT, L.H])
            L.gated = [sb(f"gated{n}{h}", [P, NT, N]) for h in range(L.H)]
            L.prob = [sb(f"prob{n}{h}", [P, NT, N]) for h in range(L.H)]
            L.probT = [sb(f"probT{n}{h}", [P, NT, N]) for h in range(L.H)]
            L.rden = sb("rden" + n, [P, NT, L.H])
            L.stat = sb("stat" + n, [P, NT, 6])
            L.mv = sb("mv" + n, [P, NT, 2])
            L.ve = sb("ve" + n, [P, NT])
            L.nm = sb("nm" + n, [P, NT])
            L.rstd = sb("rstd" + n, [P, NT])
        y0 = sb("y0", [P, NT, D])
        e0 = sb("e0", [P, NT, D])
        x1 = sb("x1", [P, NT, D])
        x1b = sb("x1b", [P, NT, D])
        x1c = sb("x1c", [P, NT, D])
        hid = sb("hid", [P, NT, HD])
        ehid = sb("ehid", [P, NT, HD])
        y2 = sb("y2", [P, NT, D])
        res = sb("res", [P, NT, D])

        PS = [pb(f"PS{i}", [P, 512]) for i in range(8)]
        PSm = [p[:, :].bitcast(BF16) for p in PS]

        s_cst, s_cst2, s_cs, s_b = (sem(n) for n in ("constants", "identity_made", "colsum_summed", "biases_made"))
        s_x, s_adj, s_out = sem("x_loaded"), sem("adj_loaded"), sem("out_stored")
        s_gab, s_gbc, s_xc, s_xr = (sem(n) for n in ("gate_to_b", "gate_to_c", "x1_to_c", "residual_loaded"))
        s_g0, s_m1, s_m1d, s_mT, s_gA = (sem(n) for n in (
            "gateA_made", "masks_made", "masks_diagonal", "masks_transposed", "gates_made"))
        for L in LAYERS:
            n = L.name
            L.s_wld, L.s_wab, L.s_round, L.s_split = (
                sem(k + n) for k in ("weights_loaded_", "score_columns_", "weights_rounded_", "weights_split_"))
            nin = 2 if L is C else 1
            L.s_inT = [sem(f"inT{u}_{n}") for u in range(nin)]
            L.s_hi = [sem(f"high{u}_{n}") for u in range(nin)]
            L.s_lo = [sem(f"low{u}_{n}") for u in range(nin)]
            L.s_lin = [sem(f"lin{c}_{n}") for c in range(len(L.chunks))]
            L.s_v = [sem(f"values{c}_{n}") for c in range(len(L.chunks))]
            L.s_bca = [sem(f"bc_a{p}_{n}") for p in range(max(1, L.H // 2))]
            L.s_max = [sem(f"max{p}_{n}") for p in range(max(1, L.H // 2))]
            L.s_bias, L.s_top, L.s_lmax, L.s_shift = (sem(k + n) for k in ("bias_", "top_", "lmax_", "shift_"))
            L.s_relu = [sem(f"relu{h}_{n}") for h in range(L.H)]
            L.s_logit = [sem(f"logit{h}_{n}") for h in range(L.H)]
            L.s_exp = [sem(f"exp{h}_{n}") for h in range(L.H)]
            L.s_pT = [sem(f"probT{h}_{n}") for h in range(L.H)]
            L.s_p = [sem(f"prob{h}_{n}_done") for h in range(L.H)]
            nag = 2 if L.H == 1 else L.H
            L.s_agg = [sem(f"agg{u}_{n}") for u in range(nag)]
            L.s_den = [sem(f"den{u}_{n}") for u in range(nag)]
            L.s_norm = [sem(f"norm{u}_{n}") for u in range(nag)]
        s_fix = sem("scores_fixed_C")
        s_eexp = [sem(f"elu_exp{h}_B") for h in range(B.H)]
        s_elu = [sem(f"elu{h}_B") for h in range(B.H)]
        s_e0, s_y0, s_t0 = sem("elu_exp_A"), sem("elu_A"), sem("residual_A")
        for L in (A, C):
            L.s_st, L.s_mv, L.s_ve, L.s_rs, L.s_ln = (
                sem(k + L.name) for k in ("stats_", "meanvar_", "vareps_", "rstd_", "normed_"))
        s_x1b = sem("x1b_made")

        USES = [
            [(2, (B.s_norm[2],)), (1, (B.s_v[1],)), (2, (C.s_lo[1],)), (1, (B.s_p[0],))],
            [(2, (B.s_norm[0],)), (1, (B.s_v[3],)), (1, (B.s_relu[0], B.s_relu[1]))],
            [(0, (A.s_v[0],)), (3, (C.s_p[0],)), (3, (C.s_norm[1],))],
            [(2, (B.s_p[1],)), (0, (A.s_v[1],)), (1, (B.s_v[2],)), (0, (A.s_norm[0],)), (2, (C.s_v[0],))],
            [(0, (A.s_lo[0],)), (2, (B.s_norm[1],)), (1, (B.s_v[0],)), (3, (C.s_norm[0],))],
            [(2, (B.s_p[2],)), (2, (B.s_p[3],)), (2, (B.s_norm[3],)), (2, (C.s_lo[0],))],
            [(3, (C.s_relu[0],)), (1, (B.s_lo[0],)), (0, (A.s_p[0],)), (0, (A.s_norm[1],)), (2, (C.s_v[1],))],
            [(1, (s_gA,)), (0, (A.s_relu[0],)), (1, (B.s_relu[2], B.s_relu[3]))],
        ]

        def active(t):
            return not isinstance(t.at, int) or 0 <= t.at < NB

        def settle(eng):
            eng.wait_ge(s_cst2, 2)

        def bank_free(eng, b, s, t):
            uses = USES[b]
            k = [u[1][0] is s for u in uses].index(True)
            for back in range(1, 8 * len(uses)):
                lag, ended = uses[(k - back) % len(uses)]
                before = t.batch(lag - uses[k][0] + (len(uses) - 1 - (k - back)) // len(uses))
                if active(before):
                    for reader in ended:
                        eng.wait_ge(reader, before.this())
                    return

        def iterations(eng, body, needed):
            LAG = 4
            for i in range(LAG + 1):
                body(Turn(i))
            regs = {(k, step): eng.alloc_register(f"count{k + LAG + 1}x{step}") for k, step in needed}
            with eng.Fori(LAG + 1, NB) as i:
                counts = {}
                for k, step in needed:
                    r = regs[(k, step)]
                    eng.reg_add(r, i, k)
                    if step > 1:
                        eng.reg_mul(r, r, step)
                    counts[(k, step)] = eng.snap(r, min_val=(LAG + 1 + k) * step, max_val=(NB + k) * step)
                body(Turn(i, counts))
            for i in range(NB, NB + LAG):
                body(Turn(i))

        x_v = x.rearrange("b (n p) f -> b p n f", p=P)
        adj_v = adj.rearrange("b (n p) m -> b p n m", p=P)
        out_v = out.rearrange("b (n p) f -> b p n f", p=P)

        block = ctx.enter_context(nc.Block())

        @block.sync
        def _(sp):
            def everywhere(v):
                return v.partition_broadcast(P)

            def load_weights(L):
                if L is A:
                    sp.dma_start(raw0[:, :, :], w0.rearrange("(k p) f -> p k f", p=P)).then_inc(A.s_wld, DMA)
                    sp.dma_start(att0[:, :], everywhere(a0.rearrange("f o -> (f o)"))).then_inc(A.s_wld, DMA)
                elif L is B:
                    sp.dma_start(raw1[:, :, :], w1.rearrange("(k p) f -> p k f", p=P)).then_inc(B.s_wld, DMA)
                    sp.dma_start(att1[:, 0, :], everywhere(asrc1.rearrange("h f -> (h f)"))).then_inc(B.s_wld, DMA)
                    sp.dma_start(att1[:, 1, :], everywhere(adst1.rearrange("h f -> (h f)"))).then_inc(B.s_wld, DMA)
                    sp.dma_start(b1p[:, :], everywhere(b1)).then_inc(B.s_wld, DMA)
                else:
                    sp.dma_start(raw2[:, :, :], w2.rearrange("(k p) f -> p k f", p=P)).then_inc(C.s_wld, DMA)
                    sp.dma_start(att2[:, 0, :], everywhere(asrc2.rearrange("h f -> (h f)"))).then_inc(C.s_wld, DMA)
                    sp.dma_start(att2[:, 1, :], everywhere(adst2.rearrange("h f -> (h f)"))).then_inc(C.s_wld, DMA)
                    sp.dma_start(b2p[:, :], everywhere(b2)).then_inc(C.s_wld, DMA)

            def load_adj(t):
                if active(t):
                    if t.later:
                        sp.wait_ge(s_g0, t.last())
                        sp.wait_ge(s_m1, t.last())
                    sp.dma_start(adj_in[:, :, :], adj_v[t.at]).then_inc(s_adj, DMA)

            def load_x(t):
                if active(t):
                    if t.later:
                        sp.wait_ge(A.s_inT[0], t.last())
                    sp.dma_start(xin[:, :, :], x_v[t.at]).then_inc(s_x, DMA)

            def load_residual(t):
                if active(t):
                    if t.later:
                        sp.wait_ge(s_t0, t.last())
                    sp.dma_start(xres[:, :, :], x_v[t.at]).then_inc(s_xr, DMA)

            def gate_to_b(t):
                if active(t):
                    sp.wait_ge(s_gA, t.this())
                    if t.later:
                        for s in B.s_max:
                            sp.wait_ge(s, t.last())
                        sp.wait_ge(s_gbc, t.last(DMA))
                    sp.dma_start(B.gate[:, :, :], gates[:, :, :]).then_inc(s_gab, DMA)

            def gate_to_c(t):
                if active(t):
                    sp.wait_ge(s_gab, t.this(DMA))
                    if t.later:
                        sp.wait_ge(C.s_max[0], t.last())
                    sp.dma_start(C.gate[:, :, :], B.gate[:, :, :]).then_inc(s_gbc, DMA)

            def x1_to_c(t):
                if active(t):
                    sp.wait_ge(s_x1b, t.this())
                    if t.later:
                        for s in C.s_norm:
                            sp.wait_ge(s, t.last())
                    sp.dma_start(x1c[:, :, :], x1b[:, :, :]).then_inc(s_xc, DMA)

            def store(t):
                if active(t):
                    sp.wait_ge(C.s_ln, t.this())
                    sp.dma_start(out_v[t.at], res[:, :, :]).then_inc(s_out, DMA)

            def body(i):
                t0, t1, t2, t3, t4 = i.batch(0), i.batch(1), i.batch(2), i.batch(3), i.batch(4)
                load_x(t0)
                load_adj(t0)
                x1_to_c(t3)
                gate_to_c(t2)
                gate_to_b(t1)
                store(t4)
                load_residual(t0)
                if i.counts is None and i.at == 0:
                    load_weights(B)
                    load_weights(C)

            load_weights(A)
            iterations(sp, body, COUNTS + DMA_COUNTS)
            sp.wait_ge(s_out, DMA * NB)

        @block.gpsimd
        def _(pool):
            pool.memset(ident[:, :], 0.0).then_inc(s_cst, 1)
            pool.memset(identb[:, :], 0.0).then_inc(s_cst, 1)
            pool.memset(ones[:, :], 1.0).then_inc(s_cst, 1)
            pool.memset(power[:, :], -0.5).then_inc(s_cst, 1)
            for L in LAYERS:
                pool.memset(L.V[:, :, :, L.F + 2], 1.0).then_inc(s_cst, 1)
            pool.wait_ge(s_cst, 7)
            for m in (ident, identb):
                pool.affine_select(out=m[:, :], in_=m[:, :], compare_op=ALU.not_equal, fill=1.0, base=0,
                                   pattern=[[-1, P]], channel_multiplier=1).then_inc(s_cst2, 1)
            def biases(L, t):
                if active(t):
                    settle(pool)
                    if L is C:
                        pool.wait_ge(s_fix, t.this())
                    for s in L.s_v:
                        pool.wait_ge(s, t.this())
                    for s in L.s_relu:
                        if t.later:
                            pool.wait_ge(s, t.last())
                    pool.tensor_scalar(L.b4[:, :, :], L.V[:, :, :, 1], 4.0, 1.0, ALU.mult, ALU.mult)\
                        .then_inc(L.s_bias, 1)

            def normalise(L, t):
                if not active(t):
                    return
                src, dst = (y0, x1) if L is A else (y2, res)
                settle(pool)
                pool.wait_ge(L.s_mv, t.this())
                pool.tensor_scalar(L.nm[:, :], L.mv[:, :, 0], -1.0, 1.0, ALU.mult, ALU.mult)
                pool.tensor_scalar(L.ve[:, :], L.mv[:, :, 1], 1.0, EPS, ALU.mult, ALU.add).then_inc(L.s_ve, 1)
                pool.wait_ge(L.s_ve, t.this())
                pool.tensor_tensor(L.rstd[:, :], L.ve[:, :], power[:, :], ALU.pow).then_inc(L.s_rs, 1)
                settle(pool)
                pool.wait_ge(L.s_rs, t.this())
                if L is A:
                    if t.later:
                        pool.wait_ge(B.s_inT[0], t.last())
                    if t.later:
                        pool.wait_ge(s_x1b, t.last())
                else:
                    if t.later:
                        pool.wait_ge(s_out, t.last(DMA))
                for k in range(NT):
                    last = pool.tensor_scalar(dst[:, k, :], src[:, k, :], L.nm[:, k:k + 1], L.rstd[:, k:k + 1],
                                              ALU.add, ALU.mult)
                last.then_inc(L.s_ln, 1)

            def diagonal(t):
                if active(t):
                    settle(pool)
                    pool.wait_ge(s_m1, t.this())
                    for k in range(NT):
                        d = masks[:, k, k * P:(k + 1) * P]
                        last = pool.affine_select(out=d, in_=d, compare_op=ALU.not_equal, fill=0.0, base=0,
                                                  pattern=[[-1, P]], channel_multiplier=1)
                    last.then_inc(s_m1d, 1)

            def logit(L, h, t):
                if active(t):
                    pool.wait_ge(L.s_relu[h], t.this())
                    pool.tensor_tensor(L.prob[h][:, :, :], L.prob[h][:, :, :], L.gated[h][:, :, :], ALU.add)\
                        .then_inc(L.s_logit[h], 1)

            def keep_x1(t):
                if active(t):
                    if not t.later:
                        pool.wait_ge(s_b, 4)
                    pool.wait_ge(A.s_ln, t.this())
                    if t.later:
                        pool.wait_ge(s_xc, t.last(DMA))
                    pool.tensor_tensor(x1b[:, :, :], x1[:, :, :], b2p[:, :].unsqueeze(1).to_broadcast([P, NT, D]),
                                       ALU.add).then_inc(s_x1b, 1)

            def residual(t):
                if active(t):
                    pool.wait_ge(s_y0, t.this())
                    pool.wait_ge(s_xr, t.this(DMA))
                    pool.tensor_tensor(y0[:, :, :], y0[:, :, :], xres[:, :, :], ALU.add).then_inc(s_t0, 1)

            def body(i):
                t0, t1, t2, t3, t4 = i.batch(0), i.batch(1), i.batch(2), i.batch(3), i.batch(4)
                biases(A, t0)
                logit(A, 0, t0)
                biases(B, t1)
                normalise(C, t4)
                diagonal(t0)
                logit(B, 0, t1)
                logit(B, 1, t1)
                logit(B, 2, t1)
                residual(t0)
                logit(B, 3, t1)
                keep_x1(t1)
                biases(C, t2)
                normalise(A, t0)
                logit(C, 0, t2)

            iterations(pool, body, COUNTS + DMA_COUNTS)

        @block.scalar
        def _(act):
            def round_weights(L):
                act.wait_ge(L.s_wld, DMA * (2 if L is A else 4))
                raw = {"A": raw0, "B": raw1, "C": raw2}[L.name]
                for k in range(L.KT):
                    last = nc.scalar.activation(L.W[:, k, :, 2:L.F + 2], raw[:, k, :].rearrange("p (h f) -> p h f", h=L.H),
                                                ACT.Copy)
                last.then_inc(L.s_round, 1)
                act.wait_ge(L.s_wab, 2 * L.KT * L.H)
                act.wait_ge(L.s_round, 1)
                nc.scalar.activation(L.Wh[:, :, :, :], L.W[:, :, :, :], ACT.Copy).then_inc(L.s_round, 1)

            def high(L, u, b, t):
                if active(t):
                    act.wait_ge(L.s_inT[u], t.this())
                    for s in L.s_lin:
                        if t.later:
                            act.wait_ge(s, t.last())
                    nc.scalar.activation(L.inh[:, 2 * u:2 * u + 2, :], PS[b][:, :].rearrange("p (k n) -> p k n", k=2),
                                         ACT.Copy).then_inc(L.s_hi[u], 1)

            def values(L, c, b, t):
                if active(t):
                    tile, g = L.chunks[c]
                    act.wait_ge(L.s_lin[c], t.this())
                    for s in L.s_agg + [L.s_shift, L.s_bias]:
                        if t.later:
                            act.wait_ge(s, t.last())
                    nc.scalar.activation(L.V[:, tile, g * L.G:(g + 1) * L.G, 0:L.F + 2],
                                         PS[b][:, 0:L.G * (L.F + 2)].rearrange("p (h f) -> p h f", h=L.G), ACT.Copy)\
                        .then_inc(L.s_v[c], 1)

            def relu(L, h, b, t):
                if active(t):
                    act.wait_ge(L.s_max[h // 2], t.this())
                    act.wait_ge(L.s_bias, t.this())
                    if t.later:
                        act.wait_ge(L.s_pT[h], t.last())
                    for k in range(NT):
                        last = nc.scalar.activation(L.prob[h][:, k, :], PS[b][:, (h % 2) * N:(h % 2 + 1) * N],
                                                    ACT.Relu, bias=L.b4[:, k, h:h + 1], scale=4.0)
                    last.then_inc(L.s_relu[h], 1)

            def exp(L, h, t):
                if active(t):
                    act.wait_ge(L.s_logit[h], t.this())
                    act.wait_ge(L.s_shift, t.this())
                    for k in range(NT):
                        last = nc.scalar.activation(L.prob[h][:, k, :], L.prob[h][:, k, :], ACT.Exp,
                                                    bias=L.shift[:, k, h:h + 1], scale=SLOPE)
                    last.then_inc(L.s_exp[h], 1)

            def weights_copy(L, h, b, t):
                if active(t):
                    act.wait_ge(L.s_pT[h], t.this())
                    for s in [L.s_agg[h]] if L.H > 1 else L.s_agg:
                        if t.later:
                            act.wait_ge(s, t.last())
                    nc.scalar.activation(L.probT[h][:, :, :], PS[b][:, :].rearrange("p (k n) -> p k n", k=NT), ACT.Copy)\
                        .then_inc(L.s_p[h], 1)

            def norm_first(k, b, t):
                if active(t):
                    act.wait_ge(A.s_den[k], t.this())
                    if t.later:
                        act.wait_ge(A.s_ln, t.last())
                    nc.scalar.activation(y0[:, k, :], PS[b][:, 0:D], ACT.Identity, bias=ones[:, 0:1],
                                         scale=A.rden[:, k, :]).then_inc(A.s_norm[k], 1)

            def elu_exp_head(h, t):
                if active(t):
                    act.wait_ge(B.s_norm[h], t.this())
                    s = slice(h * B.F, (h + 1) * B.F)
                    if t.later:
                        act.wait_ge(s_elu[h], t.last())
                    nc.scalar.activation(ehid[:, :, s], hid[:, :, s], ACT.Exp, bias=minus1[:, :]).then_inc(s_eexp[h], 1)

            def elu_exp_first(t):
                if active(t):
                    if not t.later:
                        act.wait_ge(s_b, 1)
                    act.wait_ge(A.s_norm[0], t.this())
                    act.wait_ge(A.s_norm[1], t.this())
                    if t.later:
                        act.wait_ge(s_y0, t.last())
                    nc.scalar.activation(e0[:, :, :], y0[:, :, :], ACT.Exp, bias=minus1[:, :]).then_inc(s_e0, 1)

            def gates_make(b, t):
                if active(t):
                    act.wait_ge(s_mT, t.this())
                    if t.later:
                        act.wait_ge(s_gab, t.last(DMA))
                    nc.scalar.activation(gates[:, :, :], PSm[b][:, 0:NT * N].rearrange("p (k n) -> p k n", k=NT),
                                         ACT.Copy).then_inc(s_gA, 1)

            def body(i):
                t0, t1, t2, t3, t4 = i.batch(0), i.batch(1), i.batch(2), i.batch(3), i.batch(4)
                high(A, 0, 4, t0)
                exp(B, 3, t2)
                relu(C, 0, 6, t3)
                values(A, 0, 2, t0)
                gates_make(7, t1)
                elu_exp_head(0, t2)
                high(B, 0, 6, t1)
                values(A, 1, 3, t0)
                exp(C, 0, t3)
                elu_exp_head(1, t2)
                elu_exp_head(2, t2)
                values(B, 1, 0, t1)
                relu(A, 0, 7, t0)
                values(B, 2, 3, t1)
                elu_exp_head(3, t2)
                values(B, 3, 1, t1)
                values(B, 0, 4, t1)
                weights_copy(C, 0, 2, t3)
                exp(A, 0, t0)
                high(C, 0, 5, t2)
                high(C, 1, 0, t2)
                weights_copy(A, 0, 6, t0)
                relu(B, 0, 1, t1)
                relu(B, 1, 1, t1)
                relu(B, 2, 7, t1)
                norm_first(1, 6, t0)
                norm_first(0, 3, t0)
                elu_exp_first(t0)
                exp(B, 0, t1)
                relu(B, 3, 7, t1)
                exp(B, 2, t1)
                values(C, 1, 6, t2)
                values(C, 0, 3, t2)
                exp(B, 1, t1)
                if i.counts is None and i.at == B.prepared:
                    round_weights(B)
                if i.counts is None and i.at == C.prepared:
                    round_weights(C)

            act.wait_ge(s_cst, 7)
            round_weights(A)
            iterations(act, body, COUNTS + DMA_COUNTS)

        @block.vector
        def _(dve):
            def split_weights(L):
                dve.wait_ge(L.s_wld, DMA * (2 if L is A else 4))
                n_ab = 0
                for k in range(L.KT):
                    for h in range(L.H):
                        for j in range(2):
                            s = slice(h * L.F, (h + 1) * L.F)
                            if L is A:
                                w, v = raw0[:, k, :], att0[:, (1 - j) * D:(2 - j) * D]
                            elif L is B:
                                w, v = raw1[:, k, s], att1[:, j, s]
                            else:
                                w, v = raw2[:, k, :], att2[:, j, :]
                            nc.vector.scalar_tensor_tensor(out=prod[:, j, 0:L.F], in0=w, scalar=1.0, in1=v, op0=ALU.mult,
                                                           op1=ALU.mult, accum_out=L.W[:, k, h, j:j + 1])\
                                .then_inc(L.s_wab, 1)
                            n_ab += 1
                            if n_ab > 1:
                                dve.wait_ge(L.s_wab, n_ab - 1)
                dve.wait_ge(L.s_wab, n_ab)
                dve.wait_ge(L.s_round, 2)
                nc.vector.tensor_tensor(L.Wl[:, :, :, :], L.W[:, :, :, :], L.Wh[:, :, :, :].bitcast(F32),
                                        ALU.subtract).then_inc(L.s_split, 1)

            def finish_bias():
                dve.wait_ge(s_cs, 1)
                nc.vector.tensor_copy(colsum[:, :], PS[0][:, 0:D + 2]).then_inc(s_b, 1)
                dve.wait_ge(s_b, 3)
                nc.vector.tensor_tensor(b2p[:, :], b2p[:, :], colsum[:, 2:D + 2], ALU.subtract).then_inc(s_b, 1)

            nc.vector.memset(minus1[:, :], -1.0).then_inc(s_b, 1)
            split_weights(A)

            def low(L, u, b, t):
                if active(t):
                    dve.wait_ge(L.s_hi[u], t.this())
                    for s in L.s_lin:
                        if t.later:
                            dve.wait_ge(s, t.last())
                    nc.vector.tensor_tensor(L.inl[:, 2 * u:2 * u + 2, :], PS[b][:, :].rearrange("p (k n) -> p k n", k=2),
                                            L.inh[:, 2 * u:2 * u + 2, :].bitcast(F32), ALU.subtract)\
                        .then_inc(L.s_lo[u], 1)

            def gate_make(t):
                if active(t):
                    dve.wait_ge(s_adj, t.this(DMA))
                    if t.later:
                        dve.wait_ge(A.s_max[0], t.last())
                    nc.vector.tensor_scalar(A.gate[:, :, :], adj_in[:, :, :], 0, -BIG, ALU.is_equal, ALU.mult)\
                        .then_inc(s_g0, 1)

            def masks_make(t):
                if active(t):
                    dve.wait_ge(s_adj, t.this(DMA))
                    if t.later:
                        dve.wait_ge(s_mT, t.last())
                    nc.vector.tensor_scalar(masks[:, :, :], adj_in[:, :, :], 0, -BIG, ALU.is_le, ALU.mult)\
                        .then_inc(s_m1, 1)

            def fix_scores(t):
                if active(t):
                    dve.wait_ge(C.s_v[0], t.this())
                    dve.wait_ge(C.s_v[1], t.this())
                    nc.vector.tensor_tensor(C.V[:, :, 0, 0:2], C.V[:, :, 0, 0:2],
                                            colsum[:, 0:2].unsqueeze(1).to_broadcast([P, NT, 2]), ALU.subtract)\
                        .then_inc(s_fix, 1)

            def maxima(L, p, b, t):
                if not active(t):
                    return
                settle(dve)
                dve.wait_ge(L.s_bca[p], t.this())
                if L is A:
                    dve.wait_ge(s_g0, t.this())
                elif L is B:
                    dve.wait_ge(s_gab, t.this(DMA))
                else:
                    dve.wait_ge(s_gbc, t.this(DMA))
                if t.later:
                    dve.wait_ge(L.s_top, t.last())
                    for h in range(2 * p, min(2 * p + 2, L.H)):
                        dve.wait_ge(L.s_logit[h], t.last())
                for h in range(2 * p, min(2 * p + 2, L.H)):
                    for k in range(NT):
                        last = nc.vector.tensor_tensor_reduce(
                            out=L.gated[h][:, k, :], in0=PS[b][:, (h - 2 * p) * N:(h - 2 * p + 1) * N],
                            in1=L.gate[:, k, :], scale=1.0, scalar=-3e38, op0=ALU.add, op1=ALU.max,
                            accum_out=L.amax[:, k, h:h + 1])
                last.then_inc(L.s_max[p], 1)

            def top(L, t):
                if active(t):
                    for s in L.s_max + L.s_v + ([s_fix] if L is C else []):
                        dve.wait_ge(s, t.this())
                    nc.vector.tensor_tensor(L.top[:, :, :], L.amax[:, :, :], L.V[:, :, :, 1], ALU.add).then_inc(L.s_top, 1)

            def lmax(L, t):
                if active(t):
                    dve.wait_ge(L.s_top, t.this())
                    nc.vector.scalar_tensor_tensor(out=L.lmax[:, :, :], in0=L.top[:, :, :], scalar=SLOPE,
                                                   in1=L.top[:, :, :], op0=ALU.mult, op1=ALU.max).then_inc(L.s_lmax, 1)

            def shift(L, t):
                if active(t):
                    dve.wait_ge(L.s_lmax, t.this())
                    for s in L.s_exp:
                        if t.later:
                            dve.wait_ge(s, t.last())
                    nc.vector.scalar_tensor_tensor(out=L.shift[:, :, :], in0=L.V[:, :, :, 1], scalar=SLOPE,
                                                   in1=L.lmax[:, :, :], op0=ALU.mult, op1=ALU.subtract)\
                        .then_inc(L.s_shift, 1)

            def weights_copy(L, h, b, t):
                if active(t):
                    dve.wait_ge(L.s_pT[h], t.this())
                    for s in [L.s_agg[h]] if L.H > 1 else L.s_agg:
                        if t.later:
                            dve.wait_ge(s, t.last())
                    nc.vector.tensor_copy(L.probT[h][:, :, :], PS[b][:, :].rearrange("p (k n) -> p k n", k=NT))\
                        .then_inc(L.s_p[h], 1)

            def denominator(L, u, b, t):
                if active(t):
                    dve.wait_ge(L.s_agg[u], t.this())
                    if t.later:
                        dve.wait_ge(L.s_norm[u], t.last())
                    if L is B:
                        nc.vector.reciprocal(B.rden[:, :, u], PS[b][:, 0:2 * B.F + 2]
                                             .rearrange("p (k s) -> p k s", k=2)[:, :, B.F]).then_inc(B.s_den[u], 1)
                    else:
                        nc.vector.reciprocal(L.rden[:, u, :], PS[b][:, L.F:L.F + 1]).then_inc(L.s_den[u], 1)

            def norm_head(h, b, t):
                if active(t):
                    if not t.later:
                        dve.wait_ge(s_b, 2)
                    dve.wait_ge(B.s_den[h], t.this())
                    for s in C.s_inT:
                        if t.later:
                            dve.wait_ge(s, t.last())
                    for k in range(NT):
                        o = k * (B.F + 1)
                        last = nc.vector.scalar_tensor_tensor(
                            out=hid[:, k, h * B.F:(h + 1) * B.F], in0=PS[b][:, o:o + B.F],
                            scalar=B.rden[:, k, h:h + 1], in1=b1p[:, h * B.F:(h + 1) * B.F], op0=ALU.mult, op1=ALU.add)
                    last.then_inc(B.s_norm[h], 1)

            def elu_head(h, t):
                if active(t):
                    dve.wait_ge(s_eexp[h], t.this())
                    s = slice(h * B.F, (h + 1) * B.F)
                    nc.vector.scalar_tensor_tensor(out=hid[:, :, s], in0=ehid[:, :, s], scalar=1.0, in1=hid[:, :, s],
                                                   op0=ALU.min, op1=ALU.max).then_inc(s_elu[h], 1)

            def norm_last(k, b, t):
                if active(t):
                    dve.wait_ge(C.s_den[k], t.this())
                    if t.later:
                        dve.wait_ge(C.s_ln, t.last())
                    dve.wait_ge(s_xc, t.this(DMA))
                    nc.vector.scalar_tensor_tensor(out=y2[:, k, :], in0=PS[b][:, 0:D], scalar=C.rden[:, k, :],
                                                   in1=x1c[:, k, :], op0=ALU.mult, op1=ALU.add)\
                        .then_inc(C.s_norm[k], 1)

            def elu_first(t):
                if active(t):
                    dve.wait_ge(s_e0, t.this())
                    nc.vector.scalar_tensor_tensor(out=y0[:, :, :], in0=e0[:, :, :], scalar=1.0, in1=y0[:, :, :],
                                                   op0=ALU.min, op1=ALU.max).then_inc(s_y0, 1)

            def stats(L, t):
                if active(t):
                    if L is A:
                        dve.wait_ge(s_t0, t.this())
                    else:
                        for s in C.s_norm:
                            dve.wait_ge(s, t.this())
                    if t.later:
                        dve.wait_ge(L.s_mv, t.last())
                    for k in range(NT):
                        last = nc.vector.bn_stats(L.stat[:, k, :], (y0 if L is A else y2)[:, k, :])
                    last.then_inc(L.s_st, 1)

            def meanvar(L, t):
                if active(t):
                    settle(dve)
                    dve.wait_ge(L.s_st, t.this())
                    if t.later:
                        dve.wait_ge(L.s_ln, t.last())
                    for k in range(NT):
                        last = nc.vector.bn_aggr(L.mv[:, k, :], L.stat[:, k, :])
                    last.then_inc(L.s_mv, 1)

            def body(i):
                t0, t1, t2, t3, t4 = i.batch(0), i.batch(1), i.batch(2), i.batch(3), i.batch(4)
                norm_last(0, 4, t4)
                elu_first(t1)
                stats(C, t4)
                gate_make(t0)
                weights_copy(B, 0, 0, t2)
                stats(A, t1)
                fix_scores(t3)
                weights_copy(B, 2, 5, t2)
                meanvar(A, t1)
                denominator(B, 0, 1, t2)
                low(A, 0, 4, t0)
                maxima(C, 0, 6, t3)
                weights_copy(B, 1, 3, t2)
                top(C, t3)
                denominator(B, 2, 0, t2)
                norm_head(0, 1, t2)
                lmax(C, t3)
                weights_copy(B, 3, 5, t2)
                shift(C, t3)
                denominator(B, 1, 4, t2)
                norm_head(2, 0, t2)
                norm_head(1, 4, t2)
                low(B, 0, 6, t1)
                denominator(B, 3, 5, t2)
                maxima(A, 0, 7, t0)
                elu_head(0, t2)
                norm_head(3, 5, t2)
                elu_head(1, t2)
                top(A, t0)
                elu_head(2, t2)
                masks_make(t0)
                lmax(A, t0)
                elu_head(3, t2)
                meanvar(C, t4)
                shift(A, t0)
                maxima(B, 0, 1, t1)
                maxima(B, 1, 7, t1)
                low(C, 0, 5, t2)
                denominator(A, 1, 6, t0)
                low(C, 1, 0, t2)
                denominator(A, 0, 3, t0)
                top(B, t1)
                denominator(C, 1, 2, t3)
                lmax(B, t1)
                norm_last(1, 2, t3)
                denominator(C, 0, 4, t3)
                shift(B, t1)
                if i.counts is None and i.at == B.prepared:
                    split_weights(B)
                    nc.vector.tensor_scalar(b1p[:, :], b1p[:, :], 1.0, None, ALU.add).then_inc(s_b, 1)
                if i.counts is None and i.at == C.prepared:
                    split_weights(C)
                    finish_bias()

            iterations(dve, body, COUNTS + DMA_COUNTS)

        @block.tensor
        def _(pe):
            pe.wait_ge(s_cst, 7)
            pe.wait_ge(s_cst2, 2)

            def column_sums():
                pe.wait_ge(C.s_split, 1)
                for lag, ended in USES[0]:
                    for reader in ended:
                        if C.prepared >= lag:
                            pe.wait_ge(reader, C.prepared - lag + 1)
                for k in range(C.KT):
                    last = nc.tensor.matmul(PS[0][:, 0:D + 2], ones[:, :], C.W[:, k, 0, :], start=(k == 0),
                                            stop=(k == C.KT - 1))
                last.then_inc(s_cs, 1)
                pe.wait_ge(s_b, 3)

            def transpose_in(L, u, b, t):
                if not active(t):
                    return
                bank_free(pe, b, L.s_lo[u], t)
                if L is A:
                    pe.wait_ge(s_x, t.this(DMA))
                elif L is B:
                    pe.wait_ge(A.s_ln, t.this())
                else:
                    pe.wait_ge(s_elu[2 * u], t.this())
                    pe.wait_ge(s_elu[2 * u + 1], t.this())
                src = {"A": xin, "B": x1, "C": hid}[L.name]
                for k in range(2):
                    for n in range(NT):
                        last = nc.tensor.transpose(PS[b][:, k * N + n * P:k * N + (n + 1) * P],
                                                   src[:, n, (2 * u + k) * P:(2 * u + k + 1) * P], ident[:, :])
                last.then_inc(L.s_inT[u], 1)

            def project(L, c, b, t):
                if not active(t):
                    return
                tile, g = L.chunks[c]
                bank_free(pe, b, L.s_v[c], t)
                if not t.later:
                    pe.wait_ge(L.s_split, 1)
                for s in L.s_lo:
                    pe.wait_ge(s, t.this())
                terms = [(x_, w_, k) for k in range(L.KT) for x_, w_ in ((L.inh, L.Wh), (L.inh, L.Wl), (L.inl, L.Wh))]
                for n, (x_, w_, k) in enumerate(terms):
                    last = nc.tensor.matmul(PS[b][:, 0:L.G * (L.F + 2)], x_[:, k, tile * P:(tile + 1) * P],
                                            w_[:, k, g * L.G:(g + 1) * L.G, :].rearrange("p h f -> p (h f)"),
                                            start=(n == 0), stop=(n == len(terms) - 1))
                last.then_inc(L.s_lin[c], 1)

            def spread(b, off, column):
                return nc.tensor.transpose(PS[b][:, off:off + P], column.to_broadcast([P, P]), ident[:, :])

            def spread_a(L, p, b, t):
                if not active(t):
                    return
                bank_free(pe, b, L.s_relu[2 * p], t)
                for s in L.s_v + ([s_fix] if L is C else []):
                    pe.wait_ge(s, t.this())
                for h in range(2 * p, min(2 * p + 2, L.H)):
                    for k in range(NT):
                        last = spread(b, (h - 2 * p) * N + k * P, L.V[:, k, h, 0:1])
                last.then_inc(L.s_bca[p], 1)

            def transpose_weights(L, h, b, t):
                if not active(t):
                    return
                bank_free(pe, b, L.s_p[h], t)
                pe.wait_ge(L.s_exp[h], t.this())
                for k in range(NT):
                    for q in range(NT):
                        o = k * N + q * P
                        last = nc.tensor.transpose(PS[b][:, o:o + P], L.prob[h][:, q, k * P:(k + 1) * P], ident[:, :])
                last.then_inc(L.s_pT[h], 1)

            def weigh(L, u, b, t):
                if not active(t):
                    return
                bank_free(pe, b, L.s_norm[u], t)
                pe.wait_ge(L.s_p[u if L.H > 1 else 0], t.this())
                for h, d, off in ([(u, d, d * (L.F + 1)) for d in range(NT)] if L.H > 1 else [(0, u, 0)]):
                    for k in range(NT):
                        last = nc.tensor.matmul(PS[b][:, off:off + L.F + 1], L.probT[h][:, k, d * P:(d + 1) * P],
                                                L.V[:, k, h, 2:L.F + 3], start=(k == 0), stop=(k == NT - 1))
                last.then_inc(L.s_agg[u], 1)

            def transpose_masks(b, t):
                if not active(t):
                    return
                bank_free(pe, b, s_gA, t)
                pe.wait_ge(s_m1d, t.this())
                for k in range(NT):
                    for q in range(NT):
                        o = k * N + q * P
                        last = nc.tensor.transpose(PSm[b][:, o:o + P], masks[:, q, k * P:(k + 1) * P], identb[:, :])
                last.then_inc(s_mT, 1)

            def body(i):
                t0, t1, t2, t3, t4 = i.batch(0), i.batch(1), i.batch(2), i.batch(3), i.batch(4)
                transpose_in(A, 0, 4, t0)
                transpose_masks(7, t1)
                transpose_weights(B, 2, 5, t2)
                weigh(B, 0, 1, t2)
                spread_a(C, 0, 6, t3)
                transpose_weights(B, 1, 3, t2)
                weigh(B, 2, 0, t2)
                transpose_weights(B, 3, 5, t2)
                project(A, 0, 2, t0)
                weigh(B, 1, 4, t2)
                transpose_in(B, 0, 6, t1)
                project(A, 1, 3, t0)
                weigh(B, 3, 5, t2)
                spread_a(A, 0, 7, t0)
                project(B, 1, 0, t1)
                project(B, 2, 3, t1)
                project(B, 3, 1, t1)
                project(B, 0, 4, t1)
                transpose_weights(C, 0, 2, t3)
                transpose_in(C, 0, 5, t2)
                spread_a(B, 0, 1, t1)
                transpose_in(C, 1, 0, t2)
                spread_a(B, 1, 7, t1)
                transpose_weights(A, 0, 6, t0)
                weigh(C, 1, 2, t3)
                weigh(A, 1, 6, t0)
                weigh(A, 0, 3, t0)
                weigh(C, 0, 4, t3)
                project(C, 1, 6, t2)
                project(C, 0, 3, t2)
                transpose_weights(B, 0, 0, t1)
                if i.counts is None and i.at == C.prepared:
                    column_sums()

            iterations(pe, body, COUNTS + DMA_COUNTS)


_INS = ["x", "adj", "L0_gnn_W", "L0_gnn_a", "L1_gnn_W1", "L1_gnn_att_src1", "L1_gnn_att_dst1", "L1_gnn_b1",
        "L1_gnn_W2", "L1_gnn_att_src2", "L1_gnn_att_dst2", "L1_gnn_b2"]


def kernel(**inputs):
    import numpy as _np
    import concourse.bacc as _bacc
    from concourse import mybir as _mybir
    from concourse.bass_utils import run_bass_kernel_spmd as _run

    nc = _bacc.Bacc("TRN2", target_bir_lowering=False, num_devices=1)
    arrays, args = {}, []
    for name in _INS:
        a = _np.ascontiguousarray(inputs[name])
        arrays[f"in_{name}_dram"] = a
        args.append(nc.dram_tensor(f"in_{name}_dram", a.shape, _mybir.dt.from_np(a.dtype), kind="ExternalInput").ap())
    out = nc.dram_tensor("out_0_dram", inputs["x"].shape, F32, kind="ExternalOutput").ap()
    gat_kernel(nc, *args, out)
    r = _run(nc, [arrays], core_ids=[0])
    return r.results[0]["out_0_dram"]
```

```python
import concourse.bass as bass
from concourse import mybir
from contextlib import ExitStack

F32 = mybir.dt.float32
F32R = mybir.dt.float32r
BF16 = mybir.dt.bfloat16
I32 = mybir.dt.int32
ALU = mybir.AluOpType
ACT = mybir.ActivationFunctionType

P = 128
SLOPE = 0.2
EPS = 1e-5
BIG = 2.0 ** 100
DMA = 16


class Layer:

    def __init__(self, name, heads, width, k_tiles, per_chunk):
        self.name = name
        self.H = heads
        self.F = width
        self.KT = k_tiles
        self.G = per_chunk
        self.chunks = [(t, g) for t in range(2) for g in range(heads // per_chunk)]


class Turn:

    def __init__(self, i, counts=None, off=0):
        self.i, self.counts, self.off = i, counts, off
        self.at = i + off

    @property
    def first(self):
        return self.counts is None and self.at == 0

    def batch(self, lag):
        return Turn(self.i, self.counts, self.off - lag)

    def this(self, step=1):
        return (self.at + 1) * step if self.counts is None else self.counts[(self.off + 1, step)]

    def last(self, step=1):
        return self.at * step if self.counts is None else self.counts[(self.off, step)]

    @property
    def later(self):
        return self.counts is not None or self.at > 0


COUNTS = [(k, 1) for k in range(-4, 2)]
DMA_COUNTS = [(k, DMA) for k in range(-4, 2)]


def gat_kernel(nc, x, adj, w0, a0, w1, asrc1, adst1, b1, w2, asrc2, adst2, b2, out):
    NB, N, D = x.shape
    NT = N // P
    A = Layer("A", 1, D, D // P, 1)
    B = Layer("B", asrc1.shape[0], asrc1.shape[1], D // P, 2)
    C = Layer("C", 1, D, w2.shape[0] // P, 1)
    LAYERS = (A, B, C)
    HD = B.H * B.F

    ctx = ExitStack()
    with ctx:
        def sb(name, shape, dt=F32):
            return ctx.enter_context(nc.sbuf_tensor(name, shape, dt))

        def pb(name, shape, dt=F32):
            return ctx.enter_context(nc.psum_tensor(name, shape, dt))

        def sem(name):
            return ctx.enter_context(nc.semaphore(name))

        ident = sb("ident", [P, P])
        identb = sb("identb", [P, P], BF16)
        ones = sb("ones", [P, P])
        power = sb("power", [P, NT])
        raw0 = sb("raw0", [P, A.KT, D])
        raw1 = sb("raw1", [P, B.KT, HD])
        raw2 = sb("raw2", [P, C.KT, D])
        att0 = sb("att0", [P, 2 * D])
        att1 = sb("att1", [P, 2, HD])
        att2 = sb("att2", [P, 2, D])
        b1p = sb("b1p", [P, HD])
        b2p = sb("b2p", [P, D])
        colsum = sb("colsum", [P, D + 2])
        prod = sb("prod", [P, 2, D])
        minus1 = sb("minus1", [P, 1])
        for L in LAYERS:
            L.W = sb("W" + L.name, [P, L.KT, L.H, L.F + 2])
            L.Wh = sb("Wh" + L.name, [P, L.KT, L.H, L.F + 2], F32R)
            L.Wl = sb("Wl" + L.name, [P, L.KT, L.H, L.F + 2], F32R)

        xin = sb("xin", [P, NT, D])
        xres = sb("xres", [P, NT, D])
        adj_in = sb("adj_in", [P, NT, N], I32)
        A.gate = sb("gateA", [P, NT, N], BF16)
        masks = sb("masks", [P, NT, N], BF16)
        gates = sb("gates", [P, NT, N], BF16)
        B.gate = sb("gateB", [P, NT, N], BF16)
        C.gate = sb("gateC", [P, NT, N], BF16)
        for L in LAYERS:
            n = L.name
            L.inh = sb("inh" + n, [P, L.KT, N], F32R)
            L.inl = sb("inl" + n, [P, L.KT, N], F32R)
            L.V = sb("V" + n, [P, NT, L.H, L.F + 3])
            L.amax = sb("amax" + n, [P, NT, L.H])
            L.top = sb("top" + n, [P, NT, L.H])
            L.lmax = sb("lmax" + n, [P, NT, L.H])
            L.shift = sb("shift" + n, [P, NT, L.H])
            L.b4 = sb("b4" + n, [P, NT, L.H])
            L.gated = [sb(f"gated{n}{h}", [P, NT, N]) for h in range(L.H)]
            L.prob = [sb(f"prob{n}{h}", [P, NT, N]) for h in range(L.H)]
            L.probT = [sb(f"probT{n}{h}", [P, NT, N]) for h in range(L.H)]
            L.rden = sb("rden" + n, [P, NT, L.H])
            L.stat = sb("stat" + n, [P, NT, 6])
            L.mv = sb("mv" + n, [P, NT, 2])
            L.ve = sb("ve" + n, [P, NT])
            L.nm = sb("nm" + n, [P, NT])
            L.rstd = sb("rstd" + n, [P, NT])
        y0 = sb("y0", [P, NT, D])
        e0 = sb("e0", [P, NT, D])
        x1 = sb("x1", [P, NT, D])
        x1b = sb("x1b", [P, NT, D])
        x1c = sb("x1c", [P, NT, D])
        hid = sb("hid", [P, NT, HD])
        ehid = sb("ehid", [P, NT, HD])
        y2 = sb("y2", [P, NT, D])
        res = sb("res", [P, NT, D])

        PS = [pb(f"PS{i}", [P, 512]) for i in range(8)]
        PSm = [p[:, :].bitcast(BF16) for p in PS]

        s_cst, s_cst2, s_cs, s_b = (sem(n) for n in ("constants", "identity_made", "colsum_summed", "biases_made"))
        s_x, s_adj, s_out = sem("x_loaded"), sem("adj_loaded"), sem("out_stored")
        s_gab, s_gbc, s_xc, s_xr = (sem(n) for n in ("gate_to_b", "gate_to_c", "x1_to_c", "residual_loaded"))
        s_g0, s_m1, s_m1d, s_mT, s_gA = (sem(n) for n in (
            "gateA_made", "masks_made", "masks_diagonal", "masks_transposed", "gates_made"))
        for L in LAYERS:
            n = L.name
            L.s_wld, L.s_wab, L.s_round, L.s_split = (
                sem(k + n) for k in ("weights_loaded_", "score_columns_", "weights_rounded_", "weights_split_"))
            nin = 2 if L is C else 1
            L.s_inT = [sem(f"inT{u}_{n}") for u in range(nin)]
            L.s_hi = [sem(f"high{u}_{n}") for u in range(nin)]
            L.s_lo = [sem(f"low{u}_{n}") for u in range(nin)]
            L.s_lin = [sem(f"lin{c}_{n}") for c in range(len(L.chunks))]
            L.s_v = [sem(f"values{c}_{n}") for c in range(len(L.chunks))]
            L.s_bca = [sem(f"bc_a{p}_{n}") for p in range(max(1, L.H // 2))]
            L.s_max = [sem(f"max{p}_{n}") for p in range(max(1, L.H // 2))]
            L.s_bias, L.s_top, L.s_lmax, L.s_shift = (sem(k + n) for k in ("bias_", "top_", "lmax_", "shift_"))
            L.s_relu = [sem(f"relu{h}_{n}") for h in range(L.H)]
            L.s_logit = [sem(f"logit{h}_{n}") for h in range(L.H)]
            L.s_exp = [sem(f"exp{h}_{n}") for h in range(L.H)]
            L.s_pT = [sem(f"probT{h}_{n}") for h in range(L.H)]
            L.s_p = [sem(f"prob{h}_{n}_done") for h in range(L.H)]
            nag = 2 if L.H == 1 else L.H
            L.s_agg = [sem(f"agg{u}_{n}") for u in range(nag)]
            L.s_den = [sem(f"den{u}_{n}") for u in range(nag)]
            L.s_norm = [sem(f"norm{u}_{n}") for u in range(nag)]
        s_fix = sem("scores_fixed_C")
        s_eexp = [sem(f"elu_exp{h}_B") for h in range(B.H)]
        s_elu = [sem(f"elu{h}_B") for h in range(B.H)]
        s_e0, s_y0, s_t0 = sem("elu_exp_A"), sem("elu_A"), sem("residual_A")
        for L in (A, C):
            L.s_st, L.s_mv, L.s_ve, L.s_rs, L.s_ln = (
                sem(k + L.name) for k in ("stats_", "meanvar_", "vareps_", "rstd_", "normed_"))
        s_x1b = sem("x1b_made")

        USES = [
            [(2, (B.s_p[1],)), (0, (A.s_v[1],)), (1, (B.s_v[0],)), (2, (C.s_lo[1],))],
            [(2, (B.s_norm[0],)), (2, (C.s_lo[0],)), (2, (C.s_v[1],))],
            [(2, (B.s_p[2],)), (2, (B.s_p[3],)), (1, (B.s_v[1],)), (0, (A.s_norm[0],))],
            [(0, (A.s_v[0],)), (1, (B.s_lo[0],)), (0, (A.s_p[0],)), (0, (A.s_norm[1],)), (2, (C.s_v[0],))],
            [(0, (A.s_lo[0],)), (2, (B.s_norm[1],)), (1, (B.s_v[2],)), (1, (B.s_relu[2], B.s_relu[3]))],
            [(2, (B.s_norm[3],)), (1, (B.s_relu[0], B.s_relu[1])), (3, (C.s_norm[0],)), (0, (s_gA,))],
            [(3, (C.s_relu[0],)), (1, (B.s_v[3],)), (3, (C.s_p[0],))],
            [(2, (B.s_norm[2],)), (0, (A.s_relu[0],)), (3, (C.s_norm[1],)), (1, (B.s_p[0],))],
        ]

        def active(t):
            return not isinstance(t.at, int) or 0 <= t.at < NB

        def settle(eng):
            eng.wait_ge(s_cst2, 2)

        def bank_free(eng, b, s, t):
            uses = USES[b]
            k = [u[1][0] is s for u in uses].index(True)
            for back in range(1, 8 * len(uses)):
                lag, ended = uses[(k - back) % len(uses)]
                before = t.batch(lag - uses[k][0] + (len(uses) - 1 - (k - back)) // len(uses))
                if active(before):
                    for reader in ended:
                        eng.wait_ge(reader, before.this())
                    return

        def iterations(eng, body, needed):
            LAG = 4
            for i in range(LAG + 1):
                body(Turn(i))
            regs = {(k, step): eng.alloc_register(f"count{k + LAG + 1}x{step}") for k, step in needed}
            with eng.Fori(LAG + 1, NB) as i:
                counts = {}
                for k, step in needed:
                    r = regs[(k, step)]
                    eng.reg_add(r, i, k)
                    if step > 1:
                        eng.reg_mul(r, r, step)
                    counts[(k, step)] = eng.snap(r, min_val=(LAG + 1 + k) * step, max_val=(NB + k) * step)
                body(Turn(i, counts))
            for i in range(NB, NB + LAG):
                body(Turn(i))

        x_v = x.rearrange("b (n p) f -> b p n f", p=P)
        adj_v = adj.rearrange("b (n p) m -> b p n m", p=P)
        out_v = out.rearrange("b (n p) f -> b p n f", p=P)

        block = ctx.enter_context(nc.Block())

        @block.sync
        def _(sp):
            def load_adj(t):
                if active(t):
                    if t.later:
                        sp.wait_ge(s_g0, t.last())
                        sp.wait_ge(s_m1, t.last())
                    sp.dma_start(adj_in[:, :, :], adj_v[t.at]).then_inc(s_adj, DMA)

            def load_x(t):
                if active(t):
                    if t.later:
                        sp.wait_ge(A.s_inT[0], t.last())
                    sp.dma_start(xin[:, :, :], x_v[t.at]).then_inc(s_x, DMA)

            def load_residual(t):
                if active(t):
                    if t.later:
                        sp.wait_ge(s_t0, t.last())
                    sp.dma_start(xres[:, :, :], x_v[t.at]).then_inc(s_xr, DMA)

            def gate_to_b(t):
                if active(t):
                    sp.wait_ge(s_gA, t.this())
                    if t.later:
                        for s in B.s_max:
                            sp.wait_ge(s, t.last())
                        sp.wait_ge(s_gbc, t.last(DMA))
                    sp.dma_start(B.gate[:, :, :], gates[:, :, :]).then_inc(s_gab, DMA)

            def gate_to_c(t):
                if active(t):
                    sp.wait_ge(s_gab, t.this(DMA))
                    if t.later:
                        sp.wait_ge(C.s_max[0], t.last())
                    sp.dma_start(C.gate[:, :, :], B.gate[:, :, :]).then_inc(s_gbc, DMA)

            def x1_to_c(t):
                if active(t):
                    sp.wait_ge(s_x1b, t.this())
                    if t.later:
                        for s in C.s_norm:
                            sp.wait_ge(s, t.last())
                    sp.dma_start(x1c[:, :, :], x1b[:, :, :]).then_inc(s_xc, DMA)

            def store(t):
                if active(t):
                    sp.wait_ge(C.s_ln, t.this())
                    sp.dma_start(out_v[t.at], res[:, :, :]).then_inc(s_out, DMA)

            def body(i):
                t0, t1, t2, t3, t4 = i.batch(0), i.batch(1), i.batch(2), i.batch(3), i.batch(4)
                load_x(t0)
                load_adj(t0)
                x1_to_c(t3)
                gate_to_c(t2)
                gate_to_b(t1)
                load_residual(t0)
                store(t4)

            sp.dma_start(raw0[:, :, :], w0.rearrange("(k p) f -> p k f", p=P)).then_inc(A.s_wld, DMA)
            sp.dma_start(att0[:, :], a0.rearrange("f o -> (f o)").partition_broadcast(P)).then_inc(A.s_wld, DMA)
            iterations(sp, body, COUNTS + DMA_COUNTS)
            sp.wait_ge(s_out, DMA * NB)

        @block.gpsimd
        def _(pool):
            pool.memset(ident[:, :], 0.0).then_inc(s_cst, 1)
            pool.memset(identb[:, :], 0.0).then_inc(s_cst, 1)
            pool.memset(ones[:, :], 1.0).then_inc(s_cst, 1)
            pool.memset(power[:, :], -0.5).then_inc(s_cst, 1)
            for L in LAYERS:
                pool.memset(L.V[:, :, :, L.F + 2], 1.0).then_inc(s_cst, 1)
            pool.wait_ge(s_cst, 7)
            for m in (ident, identb):
                pool.affine_select(out=m[:, :], in_=m[:, :], compare_op=ALU.not_equal, fill=1.0, base=0,
                                   pattern=[[-1, P]], channel_multiplier=1).then_inc(s_cst2, 1)
            def biases(L, t):
                if active(t):
                    settle(pool)
                    if L is C:
                        pool.wait_ge(s_fix, t.this())
                    for s in L.s_v:
                        pool.wait_ge(s, t.this())
                    for s in L.s_relu:
                        if t.later:
                            pool.wait_ge(s, t.last())
                    pool.tensor_scalar(L.b4[:, :, :], L.V[:, :, :, 1], 4.0, 1.0, ALU.mult, ALU.mult)\
                        .then_inc(L.s_bias, 1)

            def normalise(L, t):
                if not active(t):
                    return
                src, dst = (y0, x1) if L is A else (y2, res)
                settle(pool)
                pool.wait_ge(L.s_mv, t.this())
                pool.tensor_scalar(L.nm[:, :], L.mv[:, :, 0], -1.0, 1.0, ALU.mult, ALU.mult)
                pool.tensor_scalar(L.ve[:, :], L.mv[:, :, 1], 1.0, EPS, ALU.mult, ALU.add).then_inc(L.s_ve, 1)
                pool.wait_ge(L.s_ve, t.this())
                pool.tensor_tensor(L.rstd[:, :], L.ve[:, :], power[:, :], ALU.pow).then_inc(L.s_rs, 1)
                settle(pool)
                pool.wait_ge(L.s_rs, t.this())
                if L is A:
                    if t.later:
                        pool.wait_ge(B.s_inT[0], t.last())
                    if t.later:
                        pool.wait_ge(s_x1b, t.last())
                else:
                    if t.later:
                        pool.wait_ge(s_out, t.last(DMA))
                for k in range(NT):
                    last = pool.tensor_scalar(dst[:, k, :], src[:, k, :], L.nm[:, k:k + 1], L.rstd[:, k:k + 1],
                                              ALU.add, ALU.mult)
                last.then_inc(L.s_ln, 1)

            def diagonal(t):
                if active(t):
                    settle(pool)
                    pool.wait_ge(s_m1, t.this())
                    for k in range(NT):
                        d = masks[:, k, k * P:(k + 1) * P]
                        last = pool.affine_select(out=d, in_=d, compare_op=ALU.not_equal, fill=0.0, base=0,
                                                  pattern=[[-1, P]], channel_multiplier=1)
                    last.then_inc(s_m1d, 1)

            def logit(L, h, t):
                if active(t):
                    pool.wait_ge(L.s_relu[h], t.this())
                    pool.tensor_tensor(L.prob[h][:, :, :], L.prob[h][:, :, :], L.gated[h][:, :, :], ALU.add)\
                        .then_inc(L.s_logit[h], 1)

            def keep_x1(t):
                if active(t):
                    if not t.later:
                        pool.wait_ge(s_b, 4)
                    pool.wait_ge(A.s_ln, t.this())
                    if t.later:
                        pool.wait_ge(s_xc, t.last(DMA))
                    pool.tensor_tensor(x1b[:, :, :], x1[:, :, :], b2p[:, :].unsqueeze(1).to_broadcast([P, NT, D]),
                                       ALU.add).then_inc(s_x1b, 1)

            def residual(t):
                if active(t):
                    pool.wait_ge(s_y0, t.this())
                    pool.wait_ge(s_xr, t.this(DMA))
                    pool.tensor_tensor(y0[:, :, :], y0[:, :, :], xres[:, :, :], ALU.add).then_inc(s_t0, 1)

            def body(i):
                t0, t1, t2, t3, t4 = i.batch(0), i.batch(1), i.batch(2), i.batch(3), i.batch(4)
                logit(C, 0, t3)
                diagonal(t0)
                biases(A, t0)
                logit(A, 0, t0)
                biases(B, t1)
                normalise(C, t4)
                logit(B, 0, t1)
                logit(B, 1, t1)
                logit(B, 2, t1)
                residual(t0)
                logit(B, 3, t1)
                keep_x1(t1)
                biases(C, t2)
                normalise(A, t0)

            iterations(pool, body, COUNTS + DMA_COUNTS)

        @block.scalar
        def _(act):
            def load_weights(L):
                if L is B:
                    act.dma_start(raw1[:, :, :], w1.rearrange("(k p) f -> p k f", p=P)).then_inc(B.s_wld, DMA)
                    act.dma_start(att1[:, 0, :], asrc1.rearrange("h f -> (h f)").partition_broadcast(P))\
                        .then_inc(B.s_wld, DMA)
                    act.dma_start(att1[:, 1, :], adst1.rearrange("h f -> (h f)").partition_broadcast(P))\
                        .then_inc(B.s_wld, DMA)
                    act.dma_start(b1p[:, :], b1.partition_broadcast(P)).then_inc(B.s_wld, DMA)
                else:
                    act.dma_start(raw2[:, :, :], w2.rearrange("(k p) f -> p k f", p=P)).then_inc(C.s_wld, DMA)
                    act.dma_start(att2[:, 0, :], asrc2.rearrange("h f -> (h f)").partition_broadcast(P))\
                        .then_inc(C.s_wld, DMA)
                    act.dma_start(att2[:, 1, :], adst2.rearrange("h f -> (h f)").partition_broadcast(P))\
                        .then_inc(C.s_wld, DMA)
                    act.dma_start(b2p[:, :], b2.partition_broadcast(P)).then_inc(C.s_wld, DMA)

            def copy_weights(L):
                act.wait_ge(L.s_wld, DMA * (2 if L is A else 4))
                raw = {"A": raw0, "B": raw1, "C": raw2}[L.name]
                for k in range(L.KT):
                    last = nc.scalar.activation(L.W[:, k, :, 2:L.F + 2], raw[:, k, :].rearrange("p (h f) -> p h f", h=L.H),
                                                ACT.Copy)
                last.then_inc(L.s_round, 1)

            def round_weights(L):
                act.wait_ge(L.s_wab, 2 * L.KT * L.H)
                act.wait_ge(L.s_round, 1)
                nc.scalar.activation(L.Wh[:, :, :, :], L.W[:, :, :, :], ACT.Copy).then_inc(L.s_round, 1)

            def high(L, u, b, t):
                if active(t):
                    act.wait_ge(L.s_inT[u], t.this())
                    for s in L.s_lin:
                        if t.later:
                            act.wait_ge(s, t.last())
                    nc.scalar.activation(L.inh[:, 2 * u:2 * u + 2, :], PS[b][:, :].rearrange("p (k n) -> p k n", k=2),
                                         ACT.Copy).then_inc(L.s_hi[u], 1)

            def values(L, c, b, t):
                if active(t):
                    tile, g = L.chunks[c]
                    act.wait_ge(L.s_lin[c], t.this())
                    for s in L.s_agg + [L.s_shift, L.s_bias]:
                        if t.later:
                            act.wait_ge(s, t.last())
                    nc.scalar.activation(L.V[:, tile, g * L.G:(g + 1) * L.G, 0:L.F + 2],
                                         PS[b][:, 0:L.G * (L.F + 2)].rearrange("p (h f) -> p h f", h=L.G), ACT.Copy)\
                        .then_inc(L.s_v[c], 1)

            def relu(L, h, b, t):
                if active(t):
                    act.wait_ge(L.s_max[h // 2], t.this())
                    act.wait_ge(L.s_bias, t.this())
                    if t.later:
                        act.wait_ge(L.s_pT[h], t.last())
                    for k in range(NT):
                        last = nc.scalar.activation(L.prob[h][:, k, :], PS[b][:, (h % 2) * N:(h % 2 + 1) * N],
                                                    ACT.Relu, bias=L.b4[:, k, h:h + 1], scale=4.0)
                    last.then_inc(L.s_relu[h], 1)

            def exp(L, h, t):
                if active(t):
                    act.wait_ge(L.s_logit[h], t.this())
                    act.wait_ge(L.s_shift, t.this())
                    for k in range(NT):
                        last = nc.scalar.activation(L.prob[h][:, k, :], L.prob[h][:, k, :], ACT.Exp,
                                                    bias=L.shift[:, k, h:h + 1], scale=SLOPE)
                    last.then_inc(L.s_exp[h], 1)

            def weights_copy(L, h, b, t):
                if active(t):
                    act.wait_ge(L.s_pT[h], t.this())
                    for s in [L.s_agg[h]] if L.H > 1 else L.s_agg:
                        if t.later:
                            act.wait_ge(s, t.last())
                    nc.scalar.activation(L.probT[h][:, :, :], PS[b][:, :].rearrange("p (k n) -> p k n", k=NT), ACT.Copy)\
                        .then_inc(L.s_p[h], 1)

            def norm_first(k, b, t):
                if active(t):
                    act.wait_ge(A.s_den[k], t.this())
                    if t.later:
                        act.wait_ge(A.s_ln, t.last())
                    nc.scalar.activation(y0[:, k, :], PS[b][:, 0:D], ACT.Identity, bias=ones[:, 0:1],
                                         scale=A.rden[:, k, :]).then_inc(A.s_norm[k], 1)

            def elu_exp_head(h, t):
                if active(t):
                    act.wait_ge(B.s_norm[h], t.this())
                    s = slice(h * B.F, (h + 1) * B.F)
                    if t.later:
                        act.wait_ge(s_elu[h], t.last())
                    nc.scalar.activation(ehid[:, :, s], hid[:, :, s], ACT.Exp, bias=minus1[:, :]).then_inc(s_eexp[h], 1)

            def elu_exp_first(t):
                if active(t):
                    if not t.later:
                        act.wait_ge(s_b, 1)
                    act.wait_ge(A.s_norm[0], t.this())
                    act.wait_ge(A.s_norm[1], t.this())
                    if t.later:
                        act.wait_ge(s_y0, t.last())
                    nc.scalar.activation(e0[:, :, :], y0[:, :, :], ACT.Exp, bias=minus1[:, :]).then_inc(s_e0, 1)

            def gates_make(b, t):
                if active(t):
                    act.wait_ge(s_mT, t.this())
                    if t.later:
                        act.wait_ge(s_gab, t.last(DMA))
                    nc.scalar.activation(gates[:, :, :], PSm[b][:, 0:NT * N].rearrange("p (k n) -> p k n", k=NT),
                                         ACT.Copy).then_inc(s_gA, 1)

            def body(i):
                t0, t1, t2, t3, t4 = i.batch(0), i.batch(1), i.batch(2), i.batch(3), i.batch(4)
                high(A, 0, 4, t0)
                gates_make(5, t1)
                exp(B, 3, t2)
                values(A, 0, 3, t0)
                relu(C, 0, 6, t3)
                elu_exp_head(0, t2)
                high(B, 0, 3, t1)
                values(A, 1, 0, t0)
                if i.first:
                    copy_weights(B)
                exp(C, 0, t3)
                elu_exp_head(2, t2)
                elu_exp_head(1, t2)
                values(B, 1, 2, t1)
                relu(A, 0, 7, t0)
                if i.first:
                    round_weights(B)
                values(B, 3, 6, t1)
                elu_exp_head(3, t2)
                values(B, 2, 4, t1)
                values(B, 0, 0, t1)
                weights_copy(C, 0, 6, t3)
                exp(A, 0, t0)
                if i.first:
                    copy_weights(C)
                high(C, 0, 1, t2)
                high(C, 1, 0, t2)
                weights_copy(A, 0, 3, t0)
                if i.first:
                    round_weights(C)
                relu(B, 0, 5, t1)
                relu(B, 1, 5, t1)
                relu(B, 2, 4, t1)
                norm_first(1, 3, t0)
                norm_first(0, 2, t0)
                elu_exp_first(t0)
                exp(B, 0, t1)
                relu(B, 3, 4, t1)
                exp(B, 2, t1)
                values(C, 1, 1, t2)
                values(C, 0, 3, t2)
                exp(B, 1, t1)
            act.wait_ge(s_cst, 7)
            copy_weights(A)
            load_weights(B)
            load_weights(C)
            round_weights(A)
            iterations(act, body, COUNTS + DMA_COUNTS)

        @block.vector
        def _(dve):
            def score_columns(L):
                dve.wait_ge(L.s_wld, DMA * (2 if L is A else 4))
                n_ab = 0
                for k in range(L.KT):
                    for h in range(L.H):
                        for j in range(2):
                            s = slice(h * L.F, (h + 1) * L.F)
                            if L is A:
                                w, v = raw0[:, k, :], att0[:, (1 - j) * D:(2 - j) * D]
                            elif L is B:
                                w, v = raw1[:, k, s], att1[:, j, s]
                            else:
                                w, v = raw2[:, k, :], att2[:, j, :]
                            nc.vector.scalar_tensor_tensor(out=prod[:, j, 0:L.F], in0=w, scalar=1.0, in1=v, op0=ALU.mult,
                                                           op1=ALU.mult, accum_out=L.W[:, k, h, j:j + 1])\
                                .then_inc(L.s_wab, 1)
                            n_ab += 1
                            if n_ab > 1:
                                dve.wait_ge(L.s_wab, n_ab - 1)
                dve.wait_ge(L.s_wab, n_ab)

            def split_weights(L):
                dve.wait_ge(L.s_round, 2)
                nc.vector.tensor_tensor(L.Wl[:, :, :, :], L.W[:, :, :, :], L.Wh[:, :, :, :].bitcast(F32),
                                        ALU.subtract).then_inc(L.s_split, 1)

            def finish_b1():
                nc.vector.tensor_scalar(b1p[:, :], b1p[:, :], 1.0, None, ALU.add).then_inc(s_b, 1)

            def finish_b2():
                dve.wait_ge(s_cs, 1)
                nc.vector.tensor_copy(colsum[:, :], PS[0][:, 0:D + 2]).then_inc(s_b, 1)
                dve.wait_ge(s_b, 3)
                nc.vector.tensor_tensor(b2p[:, :], b2p[:, :], colsum[:, 2:D + 2], ALU.subtract).then_inc(s_b, 1)

            nc.vector.memset(minus1[:, :], -1.0).then_inc(s_b, 1)
            score_columns(A)
            split_weights(A)

            def low(L, u, b, t):
                if active(t):
                    dve.wait_ge(L.s_hi[u], t.this())
                    for s in L.s_lin:
                        if t.later:
                            dve.wait_ge(s, t.last())
                    nc.vector.tensor_tensor(L.inl[:, 2 * u:2 * u + 2, :], PS[b][:, :].rearrange("p (k n) -> p k n", k=2),
                                            L.inh[:, 2 * u:2 * u + 2, :].bitcast(F32), ALU.subtract)\
                        .then_inc(L.s_lo[u], 1)

            def gate_make(t):
                if active(t):
                    dve.wait_ge(s_adj, t.this(DMA))
                    if t.later:
                        dve.wait_ge(A.s_max[0], t.last())
                    nc.vector.tensor_scalar(A.gate[:, :, :], adj_in[:, :, :], 0, -BIG, ALU.is_equal, ALU.mult)\
                        .then_inc(s_g0, 1)

            def masks_make(t):
                if active(t):
                    dve.wait_ge(s_adj, t.this(DMA))
                    if t.later:
                        dve.wait_ge(s_mT, t.last())
                    nc.vector.tensor_scalar(masks[:, :, :], adj_in[:, :, :], 0, -BIG, ALU.is_le, ALU.mult)\
                        .then_inc(s_m1, 1)

            def fix_scores(t):
                if active(t):
                    dve.wait_ge(C.s_v[0], t.this())
                    dve.wait_ge(C.s_v[1], t.this())
                    nc.vector.tensor_tensor(C.V[:, :, 0, 0:2], C.V[:, :, 0, 0:2],
                                            colsum[:, 0:2].unsqueeze(1).to_broadcast([P, NT, 2]), ALU.subtract)\
                        .then_inc(s_fix, 1)

            def maxima(L, p, b, t):
                if not active(t):
                    return
                settle(dve)
                dve.wait_ge(L.s_bca[p], t.this())
                if L is A:
                    dve.wait_ge(s_g0, t.this())
                elif L is B:
                    dve.wait_ge(s_gab, t.this(DMA))
                else:
                    dve.wait_ge(s_gbc, t.this(DMA))
                if t.later:
                    dve.wait_ge(L.s_top, t.last())
                    for h in range(2 * p, min(2 * p + 2, L.H)):
                        dve.wait_ge(L.s_logit[h], t.last())
                for h in range(2 * p, min(2 * p + 2, L.H)):
                    for k in range(NT):
                        last = nc.vector.tensor_tensor_reduce(
                            out=L.gated[h][:, k, :], in0=PS[b][:, (h - 2 * p) * N:(h - 2 * p + 1) * N],
                            in1=L.gate[:, k, :], scale=1.0, scalar=-3e38, op0=ALU.add, op1=ALU.max,
                            accum_out=L.amax[:, k, h:h + 1])
                last.then_inc(L.s_max[p], 1)

            def top(L, t):
                if active(t):
                    for s in L.s_max + L.s_v + ([s_fix] if L is C else []):
                        dve.wait_ge(s, t.this())
                    nc.vector.tensor_tensor(L.top[:, :, :], L.amax[:, :, :], L.V[:, :, :, 1], ALU.add).then_inc(L.s_top, 1)

            def lmax(L, t):
                if active(t):
                    dve.wait_ge(L.s_top, t.this())
                    nc.vector.scalar_tensor_tensor(out=L.lmax[:, :, :], in0=L.top[:, :, :], scalar=SLOPE,
                                                   in1=L.top[:, :, :], op0=ALU.mult, op1=ALU.max).then_inc(L.s_lmax, 1)

            def shift(L, t):
                if active(t):
                    dve.wait_ge(L.s_lmax, t.this())
                    for s in L.s_exp:
                        if t.later:
                            dve.wait_ge(s, t.last())
                    nc.vector.scalar_tensor_tensor(out=L.shift[:, :, :], in0=L.V[:, :, :, 1], scalar=SLOPE,
                                                   in1=L.lmax[:, :, :], op0=ALU.mult, op1=ALU.subtract)\
                        .then_inc(L.s_shift, 1)

            def weights_copy(L, h, b, t):
                if active(t):
                    dve.wait_ge(L.s_pT[h], t.this())
                    for s in [L.s_agg[h]] if L.H > 1 else L.s_agg:
                        if t.later:
                            dve.wait_ge(s, t.last())
                    nc.vector.tensor_copy(L.probT[h][:, :, :], PS[b][:, :].rearrange("p (k n) -> p k n", k=NT))\
                        .then_inc(L.s_p[h], 1)

            def denominator(L, u, b, t):
                if active(t):
                    dve.wait_ge(L.s_agg[u], t.this())
                    if t.later:
                        dve.wait_ge(L.s_norm[u], t.last())
                    if L is B:
                        nc.vector.reciprocal(B.rden[:, :, u], PS[b][:, 0:2 * B.F + 2]
                                             .rearrange("p (k s) -> p k s", k=2)[:, :, B.F]).then_inc(B.s_den[u], 1)
                    else:
                        nc.vector.reciprocal(L.rden[:, u, :], PS[b][:, L.F:L.F + 1]).then_inc(L.s_den[u], 1)

            def norm_head(h, b, t):
                if active(t):
                    if not t.later:
                        dve.wait_ge(s_b, 2)
                    dve.wait_ge(B.s_den[h], t.this())
                    for s in C.s_inT:
                        if t.later:
                            dve.wait_ge(s, t.last())
                    for k in range(NT):
                        o = k * (B.F + 1)
                        last = nc.vector.scalar_tensor_tensor(
                            out=hid[:, k, h * B.F:(h + 1) * B.F], in0=PS[b][:, o:o + B.F],
                            scalar=B.rden[:, k, h:h + 1], in1=b1p[:, h * B.F:(h + 1) * B.F], op0=ALU.mult, op1=ALU.add)
                    last.then_inc(B.s_norm[h], 1)

            def elu_head(h, t):
                if active(t):
                    dve.wait_ge(s_eexp[h], t.this())
                    s = slice(h * B.F, (h + 1) * B.F)
                    nc.vector.scalar_tensor_tensor(out=hid[:, :, s], in0=ehid[:, :, s], scalar=1.0, in1=hid[:, :, s],
                                                   op0=ALU.min, op1=ALU.max).then_inc(s_elu[h], 1)

            def norm_last(k, b, t):
                if active(t):
                    dve.wait_ge(C.s_den[k], t.this())
                    if t.later:
                        dve.wait_ge(C.s_ln, t.last())
                    dve.wait_ge(s_xc, t.this(DMA))
                    nc.vector.scalar_tensor_tensor(out=y2[:, k, :], in0=PS[b][:, 0:D], scalar=C.rden[:, k, :],
                                                   in1=x1c[:, k, :], op0=ALU.mult, op1=ALU.add)\
                        .then_inc(C.s_norm[k], 1)

            def elu_first(t):
                if active(t):
                    dve.wait_ge(s_e0, t.this())
                    nc.vector.scalar_tensor_tensor(out=y0[:, :, :], in0=e0[:, :, :], scalar=1.0, in1=y0[:, :, :],
                                                   op0=ALU.min, op1=ALU.max).then_inc(s_y0, 1)

            def stats(L, t):
                if active(t):
                    if L is A:
                        dve.wait_ge(s_t0, t.this())
                    else:
                        for s in C.s_norm:
                            dve.wait_ge(s, t.this())
                    if t.later:
                        dve.wait_ge(L.s_mv, t.last())
                    for k in range(NT):
                        last = nc.vector.bn_stats(L.stat[:, k, :], (y0 if L is A else y2)[:, k, :])
                    last.then_inc(L.s_st, 1)

            def meanvar(L, t):
                if active(t):
                    settle(dve)
                    dve.wait_ge(L.s_st, t.this())
                    if t.later:
                        dve.wait_ge(L.s_ln, t.last())
                    for k in range(NT):
                        last = nc.vector.bn_aggr(L.mv[:, k, :], L.stat[:, k, :])
                    last.then_inc(L.s_mv, 1)

            def body(i):
                t0, t1, t2, t3, t4 = i.batch(0), i.batch(1), i.batch(2), i.batch(3), i.batch(4)
                gate_make(t0)
                weights_copy(B, 0, 7, t2)
                stats(A, t1)
                fix_scores(t3)
                weights_copy(B, 2, 2, t2)
                meanvar(A, t1)
                low(A, 0, 4, t0)
                if i.first:
                    score_columns(B)
                maxima(C, 0, 6, t3)
                weights_copy(B, 1, 0, t2)
                denominator(B, 0, 1, t2)
                top(C, t3)
                denominator(B, 2, 7, t2)
                masks_make(t0)
                norm_head(0, 1, t2)
                weights_copy(B, 3, 2, t2)
                lmax(C, t3)
                denominator(B, 1, 4, t2)
                shift(C, t3)
                norm_head(2, 7, t2)
                low(B, 0, 3, t1)
                norm_head(1, 4, t2)
                denominator(B, 3, 5, t2)
                maxima(A, 0, 7, t0)
                elu_head(0, t2)
                norm_head(3, 5, t2)
                elu_head(1, t2)
                top(A, t0)
                elu_head(2, t2)
                elu_head(3, t2)
                lmax(A, t0)
                meanvar(C, t4)
                shift(A, t0)
                if i.first:
                    score_columns(C)
                    split_weights(B)
                    finish_b1()
                    split_weights(C)
                maxima(B, 0, 5, t1)
                maxima(B, 1, 4, t1)
                low(C, 0, 1, t2)
                denominator(A, 1, 3, t0)
                low(C, 1, 0, t2)
                denominator(A, 0, 2, t0)
                top(B, t1)
                denominator(C, 1, 7, t3)
                norm_last(1, 7, t3)
                lmax(B, t1)
                denominator(C, 0, 5, t3)
                shift(B, t1)
                norm_last(0, 5, t3)
                elu_first(t0)
                stats(C, t3)
                if i.first:
                    finish_b2()

            iterations(dve, body, COUNTS + DMA_COUNTS)

        @block.tensor
        def _(pe):
            pe.wait_ge(s_cst, 7)
            pe.wait_ge(s_cst2, 2)

            def column_sums():
                pe.wait_ge(C.s_wab, 2 * C.KT)
                pe.wait_ge(C.s_round, 1)
                for lag, ended in USES[0]:
                    if lag == 0:
                        for reader in ended:
                            pe.wait_ge(reader, 1)
                for k in range(C.KT):
                    last = nc.tensor.matmul(PS[0][:, 0:D + 2], ones[:, :], C.W[:, k, 0, :], start=(k == 0),
                                            stop=(k == C.KT - 1))
                last.then_inc(s_cs, 1)
                pe.wait_ge(s_b, 3)

            def transpose_in(L, u, b, t):
                if not active(t):
                    return
                bank_free(pe, b, L.s_lo[u], t)
                if L is A:
                    pe.wait_ge(s_x, t.this(DMA))
                elif L is B:
                    pe.wait_ge(A.s_ln, t.this())
                else:
                    pe.wait_ge(s_elu[2 * u], t.this())
                    pe.wait_ge(s_elu[2 * u + 1], t.this())
                src = {"A": xin, "B": x1, "C": hid}[L.name]
                for k in range(2):
                    for n in range(NT):
                        last = nc.tensor.transpose(PS[b][:, k * N + n * P:k * N + (n + 1) * P],
                                                   src[:, n, (2 * u + k) * P:(2 * u + k + 1) * P], ident[:, :])
                last.then_inc(L.s_inT[u], 1)

            def project(L, c, b, t):
                if not active(t):
                    return
                tile, g = L.chunks[c]
                bank_free(pe, b, L.s_v[c], t)
                if not t.later:
                    pe.wait_ge(L.s_split, 1)
                for s in L.s_lo:
                    pe.wait_ge(s, t.this())
                terms = [(x_, w_, k) for k in range(L.KT) for x_, w_ in ((L.inh, L.Wh), (L.inh, L.Wl), (L.inl, L.Wh))]
                for n, (x_, w_, k) in enumerate(terms):
                    last = nc.tensor.matmul(PS[b][:, 0:L.G * (L.F + 2)], x_[:, k, tile * P:(tile + 1) * P],
                                            w_[:, k, g * L.G:(g + 1) * L.G, :].rearrange("p h f -> p (h f)"),
                                            start=(n == 0), stop=(n == len(terms) - 1))
                last.then_inc(L.s_lin[c], 1)

            def spread(b, off, column):
                return nc.tensor.transpose(PS[b][:, off:off + P], column.to_broadcast([P, P]), ident[:, :])

            def spread_a(L, p, b, t):
                if not active(t):
                    return
                bank_free(pe, b, L.s_relu[2 * p], t)
                for s in L.s_v + ([s_fix] if L is C else []):
                    pe.wait_ge(s, t.this())
                for h in range(2 * p, min(2 * p + 2, L.H)):
                    for k in range(NT):
                        last = spread(b, (h - 2 * p) * N + k * P, L.V[:, k, h, 0:1])
                last.then_inc(L.s_bca[p], 1)

            def transpose_weights(L, h, b, t):
                if not active(t):
                    return
                bank_free(pe, b, L.s_p[h], t)
                pe.wait_ge(L.s_exp[h], t.this())
                for k in range(NT):
                    for q in range(NT):
                        o = k * N + q * P
                        last = nc.tensor.transpose(PS[b][:, o:o + P], L.prob[h][:, q, k * P:(k + 1) * P], ident[:, :])
                last.then_inc(L.s_pT[h], 1)

            def weigh(L, u, b, t):
                if not active(t):
                    return
                bank_free(pe, b, L.s_norm[u], t)
                pe.wait_ge(L.s_p[u if L.H > 1 else 0], t.this())
                for h, d, off in ([(u, d, d * (L.F + 1)) for d in range(NT)] if L.H > 1 else [(0, u, 0)]):
                    for k in range(NT):
                        last = nc.tensor.matmul(PS[b][:, off:off + L.F + 1], L.probT[h][:, k, d * P:(d + 1) * P],
                                                L.V[:, k, h, 2:L.F + 3], start=(k == 0), stop=(k == NT - 1))
                last.then_inc(L.s_agg[u], 1)

            def transpose_masks(b, t):
                if not active(t):
                    return
                bank_free(pe, b, s_gA, t)
                pe.wait_ge(s_m1d, t.this())
                for k in range(NT):
                    for q in range(NT):
                        o = k * N + q * P
                        last = nc.tensor.transpose(PSm[b][:, o:o + P], masks[:, q, k * P:(k + 1) * P], identb[:, :])
                last.then_inc(s_mT, 1)

            def body(i):
                t0, t1, t2, t3, t4 = i.batch(0), i.batch(1), i.batch(2), i.batch(3), i.batch(4)
                transpose_in(A, 0, 4, t0)
                transpose_weights(B, 2, 2, t2)
                weigh(B, 0, 1, t2)
                spread_a(C, 0, 6, t3)
                transpose_weights(B, 1, 0, t2)
                weigh(B, 2, 7, t2)
                project(A, 0, 3, t0)
                transpose_weights(B, 3, 2, t2)
                weigh(B, 1, 4, t2)
                transpose_in(B, 0, 3, t1)
                project(A, 1, 0, t0)
                weigh(B, 3, 5, t2)
                spread_a(A, 0, 7, t0)
                project(B, 1, 2, t1)
                project(B, 3, 6, t1)
                project(B, 2, 4, t1)
                project(B, 0, 0, t1)
                transpose_weights(C, 0, 6, t3)
                transpose_in(C, 0, 1, t2)
                spread_a(B, 0, 5, t1)
                transpose_in(C, 1, 0, t2)
                spread_a(B, 1, 4, t1)
                transpose_weights(A, 0, 3, t0)
                weigh(C, 1, 7, t3)
                weigh(A, 1, 3, t0)
                weigh(A, 0, 2, t0)
                weigh(C, 0, 5, t3)
                project(C, 1, 1, t2)
                project(C, 0, 3, t2)
                transpose_weights(B, 0, 7, t1)
                transpose_masks(5, t0)
                if i.first:
                    column_sums()

            iterations(pe, body, COUNTS + DMA_COUNTS)


_INS = ["x", "adj", "L0_gnn_W", "L0_gnn_a", "L1_gnn_W1", "L1_gnn_att_src1", "L1_gnn_att_dst1", "L1_gnn_b1",
        "L1_gnn_W2", "L1_gnn_att_src2", "L1_gnn_att_dst2", "L1_gnn_b2"]


def kernel(**inputs):
    import numpy as _np
    import concourse.bacc as _bacc
    from concourse import mybir as _mybir
    from concourse.bass_utils import run_bass_kernel_spmd as _run

    nc = _bacc.Bacc("TRN2", target_bir_lowering=False, num_devices=1)
    arrays, args = {}, []
    for name in _INS:
        a = _np.ascontiguousarray(inputs[name])
        arrays[f"in_{name}_dram"] = a
        args.append(nc.dram_tensor(f"in_{name}_dram", a.shape, _mybir.dt.from_np(a.dtype), kind="ExternalInput").ap())
    out = nc.dram_tensor("out_0_dram", inputs["x"].shape, F32, kind="ExternalOutput").ap()
    gat_kernel(nc, *args, out)
    r = _run(nc, [arrays], core_ids=[0])
    return r.results[0]["out_0_dram"]
```
